# Optimizing a Trainium2 kernel written in Bass

```python
import numpy as np
import jax
import jax.numpy as jnp

def _softmax(x, axis=-1):
    return jax.nn.softmax(x, axis=axis)

def _gelu(x):
    return jax.nn.gelu(x, approximate=True)

def _silu(x):
    return jax.nn.silu(x)

def _sigmoid(x):
    return jax.nn.sigmoid(x)

def _layernorm(x, axis=-1, eps=1e-05):
    m = jnp.mean(x, axis=axis, keepdims=True)
    v = jnp.var(x, axis=axis, keepdims=True)
    return (x - m) / jnp.sqrt(v + eps)

def _scatter_add(tgt, idx, src, axis=0):
    return tgt.at[idx].add(src)

def _segment_sum(src, seg, n):
    return jax.ops.segment_sum(src, seg, n)
kernel_name = 'mk_flamingo_gated_d1_seqx_r2_3f8e64'

def setup_inputs(seed: int=0):
    np.random.seed(seed)
    _w = jnp.asarray

    def _rec_inputs():
        import jax
        import jax.numpy as jnp
        _rk = jax.random.key(seed)
        x = -0.0002928 + 1 * jax.random.normal(jax.random.fold_in(_rk, 1), (16, 512, 512), jnp.float32)
        _lenS = 512 - jax.random.randint(jax.random.fold_in(_rk, 7), (16,), 0, max(1, 512 // 4) + 1, jnp.int32)
        _lenS2 = 512 - jax.random.randint(jax.random.fold_in(_rk, 8), (16,), 0, max(1, 512 // 4) + 1, jnp.int32)
        _ctx_1024P = jax.random.normal(jax.random.fold_in(_rk, 11), (16, 16, 512), jnp.float32)
        _ctx_1024c = jax.random.dirichlet(jax.random.fold_in(_rk, 511), 0.3 * jnp.ones((16,), jnp.float32), (16, 512))
        _ctx_1024t = jnp.einsum('bsk,bkd->bsd', _ctx_1024c, _ctx_1024P)
        _ctx_1024t = _ctx_1024t * jax.lax.rsqrt(jnp.mean(jnp.square(_ctx_1024t)) + 1e-12) * 0.953939
        ctx_1024 = -1.39393e-06 + 0.999914 * (_ctx_1024t + 0.3 * jax.random.normal(jax.random.fold_in(_rk, 611), (16, 512, 512), jnp.float32))
        _g = jax.random.normal(jax.random.fold_in(_rk, 9001), (2, 1), jnp.float32)
        _g = jnp.sign(_g) * jnp.maximum(jnp.abs(_g), 1.0) + (_g == 0) * 1.0
        g_xattn = _g[0]
        g_ffn = _g[1]
        return (x, ctx_1024, g_xattn, g_ffn)
    x, ctx_1024, g_xattn, g_ffn = _rec_inputs()

    def _L0_xattn_setup():
        import jax, jax.numpy as jnp
        import numpy as np
        D_MODEL = 512
        NUM_HEADS = 16
        D_K = D_MODEL // NUM_HEADS
        B, N = (2, 1024)
        key = jax.random.key(seed)
        ks = jax.random.split(key, 11)
        s = 1.0 / np.sqrt(D_MODEL)
        inp = {'query': jax.random.normal(ks[0], (B, N, D_MODEL), jnp.float32), 'key': jax.random.normal(ks[1], (B, N, D_MODEL), jnp.float32), 'value': jax.random.normal(ks[2], (B, N, D_MODEL), jnp.float32), 'w_q': jax.random.normal(ks[3], (D_MODEL, D_MODEL), jnp.float32) * s, 'b_q': jax.random.normal(ks[4], (D_MODEL,), jnp.float32) * s, 'w_k': jax.random.normal(ks[5], (D_MODEL, D_MODEL), jnp.float32) * s, 'b_k': jax.random.normal(ks[6], (D_MODEL,), jnp.float32) * s, 'w_v': jax.random.normal(ks[7], (D_MODEL, D_MODEL), jnp.float32) * s, 'b_v': jax.random.normal(ks[8], (D_MODEL,), jnp.float32) * s, 'w_o': jax.random.normal(ks[9], (D_MODEL, D_MODEL), jnp.float32) * s, 'b_o': jax.random.normal(ks[10], (D_MODEL,), jnp.float32) * s}
        return inp
    _L0_xattn_all = _L0_xattn_setup()
    _L0_xattn_in = {k: v for k, v in _L0_xattn_all.items() if k in ('w_q', 'b_q', 'w_k', 'b_k', 'w_v', 'b_v', 'w_o', 'b_o')}
    del _L0_xattn_all

    def _L0_ffn_setup():
        import jax, jax.numpy as jnp
        import numpy as np
        E, K, D, H = (8, 2, 512, 1024)
        B, S = (1, 512)

        def _grouped_swiglu(x_sorted, counts, w1, w2, w3):
            if hasattr(jax.lax, 'ragged_dot'):
                gs = counts.astype(jnp.int32)
                h = jax.nn.silu(jax.lax.ragged_dot(x_sorted, w1, gs)) * jax.lax.ragged_dot(x_sorted, w3, gs)
                return jax.lax.ragged_dot(h, w2, gs)
            pos = jnp.arange(x_sorted.shape[0])
            eid = jnp.searchsorted(jnp.cumsum(counts), pos, side='right')
            out = jnp.zeros((x_sorted.shape[0], w2.shape[-1]), x_sorted.dtype)
            for e in range(w1.shape[0]):
                xm = jnp.where((eid == e)[:, None], x_sorted, 0.0)
                he = jax.nn.silu(xm @ w1[e]) * (xm @ w3[e])
                out = out + he @ w2[e]
            return out
        key = jax.random.key(seed)
        k0, k1, k2, k3, k4 = jax.random.split(key, 5)
        sD = 1.0 / np.sqrt(D)
        sH = 1.0 / np.sqrt(H)
        return {'hidden_states': jax.random.normal(k0, (B, S, D), jnp.float32), 'gate_w': jax.random.normal(k1, (E, D), jnp.float32) * sD, 'w1': jax.random.normal(k2, (E, D, H), jnp.float32) * sD, 'w2': jax.random.normal(k3, (E, H, D), jnp.float32) * sH, 'w3': jax.random.normal(k4, (E, D, H), jnp.float32) * sD}
    _L0_ffn_all = _L0_ffn_setup()
    _L0_ffn_in = {k: v for k, v in _L0_ffn_all.items() if k in ('gate_w', 'w1', 'w2', 'w3')}
    del _L0_ffn_all
    return {'x': x, 'ctx_1024': ctx_1024, 'g_xattn': g_xattn, 'g_ffn': g_ffn, 'L0_xattn_w_q': _L0_xattn_in['w_q'], 'L0_xattn_b_q': _L0_xattn_in['b_q'], 'L0_xattn_w_k': _L0_xattn_in['w_k'], 'L0_xattn_b_k': _L0_xattn_in['b_k'], 'L0_xattn_w_v': _L0_xattn_in['w_v'], 'L0_xattn_b_v': _L0_xattn_in['b_v'], 'L0_xattn_w_o': _L0_xattn_in['w_o'], 'L0_xattn_b_o': _L0_xattn_in['b_o'], 'L0_ffn_gate_w': _L0_ffn_in['gate_w'], 'L0_ffn_w1': _L0_ffn_in['w1'], 'L0_ffn_w2': _L0_ffn_in['w2'], 'L0_ffn_w3': _L0_ffn_in['w3']}

def reference(x, ctx_1024, g_xattn, g_ffn, L0_xattn_w_q, L0_xattn_b_q, L0_xattn_w_k, L0_xattn_b_k, L0_xattn_w_v, L0_xattn_b_v, L0_xattn_w_o, L0_xattn_b_o, L0_ffn_gate_w, L0_ffn_w1, L0_ffn_w2, L0_ffn_w3):
    import jax
    import jax.numpy as jnp

    def _L0_xattn_ref(query, key, value, w_q, b_q, w_k, b_k, w_v, b_v, w_o, b_o):
        import jax, jax.numpy as jnp
        import numpy as np
        D_MODEL = 512
        NUM_HEADS = 16
        D_K = D_MODEL // NUM_HEADS
        B, N = (2, 1024)
        Bq, Nq, _ = query.shape
        Q = (query @ w_q.T + b_q).reshape(Bq, Nq, NUM_HEADS, D_K).transpose(0, 2, 1, 3)
        K = (key @ w_k.T + b_k).reshape(Bq, -1, NUM_HEADS, D_K).transpose(0, 2, 1, 3)
        V = (value @ w_v.T + b_v).reshape(Bq, -1, NUM_HEADS, D_K).transpose(0, 2, 1, 3)
        scores = jnp.einsum('bhqd,bhkd->bhqk', Q, K) / np.sqrt(D_K).astype(np.float32)
        attn = jax.nn.softmax(scores, axis=-1)
        ctx = jnp.einsum('bhqk,bhkd->bhqd', attn, V)
        ctx = ctx.transpose(0, 2, 1, 3).reshape(Bq, Nq, D_MODEL)
        return ctx @ w_o.T + b_o

    def _L0_ffn_ref(hidden_states, gate_w, w1, w2, w3):
        import jax, jax.numpy as jnp
        import numpy as np
        E, K, D, H = (8, 2, 512, 1024)
        B, S = (1, 512)

        def _grouped_swiglu(x_sorted, counts, w1, w2, w3):
            if hasattr(jax.lax, 'ragged_dot'):
                gs = counts.astype(jnp.int32)
                h = jax.nn.silu(jax.lax.ragged_dot(x_sorted, w1, gs)) * jax.lax.ragged_dot(x_sorted, w3, gs)
                return jax.lax.ragged_dot(h, w2, gs)
            pos = jnp.arange(x_sorted.shape[0])
            eid = jnp.searchsorted(jnp.cumsum(counts), pos, side='right')
            out = jnp.zeros((x_sorted.shape[0], w2.shape[-1]), x_sorted.dtype)
            for e in range(w1.shape[0]):
                xm = jnp.where((eid == e)[:, None], x_sorted, 0.0)
                he = jax.nn.silu(xm @ w1[e]) * (xm @ w3[e])
                out = out + he @ w2[e]
            return out
        x = hidden_states.reshape(-1, D)
        N = x.shape[0]
        scores = jax.nn.softmax(x @ gate_w.T, axis=-1)
        top_scores, sel = jax.lax.top_k(scores, K)
        sel_flat = sel.T.reshape(-1)
        scores_flat = top_scores.T.reshape(-1)
        order = jnp.argsort(sel_flat, stable=True)
        tok_sorted = order % N
        scores_sorted = scores_flat[order]
        counts = jnp.bincount(sel_flat, length=E)
        x_sorted = x[tok_sorted]
        y = _grouped_swiglu(x_sorted, counts, w1, w2, w3)
        weighted = y * scores_sorted[:, None]
        out = jnp.zeros((N, D), x.dtype).at[tok_sorted].add(weighted)
        return out.reshape(hidden_states.shape)
    x = x + jnp.tanh(g_xattn[0]) * _L0_xattn_ref(_layernorm(x, axis=-1), ctx_1024, ctx_1024, L0_xattn_w_q, L0_xattn_b_q, L0_xattn_w_k, L0_xattn_b_k, L0_xattn_w_v, L0_xattn_b_v, L0_xattn_w_o, L0_xattn_b_o)
    x = x + jnp.tanh(g_ffn[0]) * _L0_ffn_ref(_layernorm(x, axis=-1), L0_ffn_gate_w, L0_ffn_w1, L0_ffn_w2, L0_ffn_w3)
    return x

_drawn_inputs = setup_inputs


def setup_inputs(seed=0):
    import zlib

    import numpy as np

    out = dict(_drawn_inputs(seed))
    spreads = {}
    factors = {'L0_xattn_b_q': 4.647, 'L0_xattn_b_k': 8.0}
    for name, (base, spread) in spreads.items():
        noise = np.random.default_rng([zlib.crc32(name.encode()), seed]).standard_normal(out[name].shape)
        drawn = base * np.exp(spread * noise) if base else spread * noise
        out[name] = jnp.asarray(drawn.astype(out[name].dtype))
    for name, factor in factors.items():
        out[name] = (out[name] * factor).astype(out[name].dtype)
    return out
```

```python
from contextlib import ExitStack

import concourse.bass as bass
from concourse import mybir

F32 = mybir.dt.float32
F32R = mybir.dt.float32r
BF16 = mybir.dt.bfloat16
I32 = mybir.dt.int32
U32 = mybir.dt.uint32
ALU = mybir.AluOpType
ACT = mybir.ActivationFunctionType
AX_X = mybir.AxisListType.X

P = 128
EPS = 1e-5
RW = 528
TILE = 256
HEADS = 16


def project_qkv(nc, x, ctx_t, wq_t, wk_t, wv_t, bq, bk, ident_dram, q_hi, q_lo, k_hi, k_lo, v_raw):
    B, S, D = x.shape
    KT = D // P
    MT = D // P
    TT = S // P

    with ExitStack() as ctx:
        def sb(name, shape, dt=F32):
            return ctx.enter_context(nc.sbuf_tensor(name, shape, dt))

        def sem(name):
            return ctx.enter_context(nc.semaphore(name))

        w_raw = sb("w_raw", [P, 3, KT, D])
        w_hi = sb("w_hi", [P, 3, KT, D], F32R)
        w_lo = sb("w_lo", [P, 3, KT, D], F32R)
        WQ, WK, WV = range(3)
        bias = sb("bias", [P, 2, MT])
        ident = sb("ident_a", [P, P])
        x_tok = sb("x_tok", [P, TT, D])
        xn = sb("xn", [P, TT, D])
        stats = sb("stats", [P, TT, 6])
        mean_sum = sb("mean_sum", [P, TT])
        mean_gap = sb("mean_gap", [P, TT])
        square_sum = sb("square_sum", [P, TT])
        mean = sb("mean", [P, TT])
        gap_square = sb("gap_square", [P, TT])
        inner_var = sb("inner_var", [P, TT])
        var_eps = sb("var_eps", [P, TT])
        rstd = sb("rstd", [P, TT])
        neg_half = sb("neg_half", [P, TT])
        ctx_raw = sb("ctx_raw", [P, KT, S])
        ctx_hi = sb("ctx_hi", [P, KT, S], F32R)
        ctx_lo = sb("ctx_lo", [P, KT, S], F32R)
        xn_hi = sb("xn_hi", [P, KT, S], F32R)
        xn_lo = sb("xn_lo", [P, KT, S], F32R)
        kst_hi = sb("kst_hi", [P, MT, S], F32R)
        kst_lo = sb("kst_lo", [P, MT, S], F32R)
        qst_hi = sb("qst_hi", [P, MT, S], F32R)
        qst_lo = sb("qst_lo", [P, MT, S], F32R)
        vst = sb("vst", [P, TT, D])
        proj = ctx.enter_context(nc.psum_tensor("proj", [P, 4, S], F32))
        turn = ctx.enter_context(nc.psum_tensor("turn", [P, KT, S], F32))

        w_loaded = sem("w_loaded")
        w_hi_ready = sem("w_hi_ready")
        w_lo_ready = sem("w_lo_ready")
        pow_const_ready = sem("pow_const_ready")
        x_loaded = sem("x_loaded")
        ctx_loaded = sem("ctx_loaded")
        stats_ready = sem("stats_ready")
        halves_ready = sem("halves_ready")
        moments_ready = sem("moments_ready")
        var_eps_ready = sem("var_eps_ready")
        rstd_ready = sem("rstd_ready")
        xn_ready = sem("xn_ready")
        ctx_hi_ready = sem("ctx_hi_ready")
        ctx_lo_ready = sem("ctx_lo_ready")
        turned = sem("turned")
        xn_hi_ready = sem("xn_hi_ready")
        xn_lo_ready = sem("xn_lo_ready")
        projected = sem("projected")
        hi_out = sem("hi_out")
        lo_out = sem("lo_out")
        v_out = sem("v_out")
        k_stored = sem("k_stored")
        q_stored = sem("q_stored")
        v_stored = sem("v_stored")

        block = ctx.enter_context(nc.Block())

        @block.sync
        def _(sp):
            for i, w in enumerate((wq_t, wk_t, wv_t)):
                sp.dma_start(w_raw[:, i], w.rearrange("(k p) n -> p k n", p=P)).then_inc(w_loaded, 16)
            sp.dma_start(bias[:, 0], bq).then_inc(w_loaded, 16)
            sp.dma_start(bias[:, 1], bk).then_inc(w_loaded, 16)
            sp.dma_start(ident[:], ident_dram).then_inc(w_loaded, 16)

            def load(b):
                sp.dma_start(ctx_raw[:], ctx_t[b].rearrange("(k p) s -> p k s", p=P)).then_inc(ctx_loaded, 16)
                sp.dma_start(x_tok[:], x[b].rearrange("(t p) d -> p t d", p=P)).then_inc(x_loaded, 16)

            def feature_rows(dram, b):
                return dram[b].rearrange("(m p) s -> p m s", p=P)

            def batch(b, last):
                if not last:
                    sp.wait_ge(ctx_hi_ready, b + 1)
                    sp.wait_ge(ctx_lo_ready, b + 1)
                    sp.wait_ge(xn_ready, TT * b + TT)
                    load(b + 1)
                sp.wait_ge(hi_out, 2 * MT * b + MT)
                sp.dma_start(feature_rows(k_hi, b), kst_hi[:].bitcast(F32)).then_inc(k_stored, 16)
                sp.wait_ge(lo_out, 2 * MT * b + MT)
                sp.dma_start(feature_rows(k_lo, b), kst_lo[:].bitcast(F32)).then_inc(k_stored, 16)
                sp.wait_ge(v_out, TT * b + TT)
                sp.dma_start(v_raw[b].rearrange("(t p) d -> p t d", p=P), vst[:]).then_inc(v_stored, 16)
                sp.wait_ge(hi_out, 2 * MT * b + 2 * MT)
                sp.dma_start(feature_rows(q_hi, b), qst_hi[:].bitcast(F32)).then_inc(q_stored, 16)
                sp.wait_ge(lo_out, 2 * MT * b + 2 * MT)
                sp.dma_start(feature_rows(q_lo, b), qst_lo[:].bitcast(F32)).then_inc(q_stored, 16)

            load(0)
            with sp.Fori(0, B - 1) as b:
                batch(b, False)
            batch(B - 1, True)
            sp.wait_ge(k_stored, 32 * B + 32)
            sp.wait_ge(q_stored, 32 * B + 32)
            sp.wait_ge(v_stored, 16 * B + 16)

        @block.gpsimd
        def _(pool):
            pool.memset(neg_half[:], -0.5).then_inc(pow_const_ready, 1)
            pool.wait_ge(pow_const_ready, 1)
            with pool.Fori(0, B) as b:
                pool.wait_ge(var_eps_ready, b + 1)
                pool.tensor_tensor(rstd[:], var_eps[:], neg_half[:], ALU.pow).then_inc(rstd_ready, 1)

        @block.scalar
        def _(act):
            act.wait_ge(w_loaded, 96)
            for i in range(3):
                act.activation(w_hi[:, i], w_raw[:, i], ACT.Copy).then_inc(w_hi_ready, 1)
            act.sem_inc(k_stored, 32)
            act.sem_inc(q_stored, 32)
            act.sem_inc(v_stored, 16)

            def split_ctx(b):
                act.wait_ge(ctx_loaded, 16 * b + 16)
                act.activation(ctx_hi[:], ctx_raw[:], ACT.Copy).then_inc(ctx_hi_ready, 1)

            def batch(b, last):
                act.wait_ge(k_stored, 32 * b + 32)
                for m in range(MT):
                    act.wait_ge(projected, 3 * MT * b + m + 1)
                    act.activation(kst_hi[:, m], proj[:, m], ACT.Identity, bias=bias[:, 1, m:m + 1]).then_inc(hi_out, 1)
                for k in range(KT):
                    act.wait_ge(turned, KT * b + k + 1)
                    act.activation(xn_hi[:, k], turn[:, k], ACT.Copy).then_inc(xn_hi_ready, 1)
                if not last:
                    act.wait_ge(projected, 3 * MT * b + 2 * MT)
                    split_ctx(b + 1)
                act.wait_ge(q_stored, 32 * b + 32)
                for m in range(MT):
                    act.wait_ge(projected, 3 * MT * b + 2 * MT + m + 1)
                    act.activation(qst_hi[:, m], proj[:, m], ACT.Identity, bias=bias[:, 0, m:m + 1]).then_inc(hi_out, 1)

            split_ctx(0)
            with act.Fori(0, B - 1) as b:
                batch(b, False)
            batch(B - 1, True)

        @block.vector
        def _(dve):
            for i in range(3):
                dve.wait_ge(w_hi_ready, i + 1)
                dve.tensor_tensor(w_lo[:, i], w_raw[:, i], w_hi[:, i].bitcast(F32), ALU.subtract).then_inc(w_lo_ready, 1)

            def split_ctx(b):
                dve.wait_ge(ctx_hi_ready, b + 1)
                dve.tensor_tensor(ctx_lo[:], ctx_raw[:], ctx_hi[:].bitcast(F32), ALU.subtract).then_inc(ctx_lo_ready, 1)

            def norm(b):
                dve.wait_ge(x_loaded, 16 * b + 16)
                for t in range(TT):
                    dve.bn_stats(stats[:, t], x_tok[:, t]).then_inc(stats_ready, 1)
                dve.wait_ge(stats_ready, TT * b + TT)
                even, odd = stats[:, :, 0:3], stats[:, :, 3:6]
                dve.tensor_tensor(mean_sum[:], even[:, :, 1], odd[:, :, 1], ALU.add).then_inc(halves_ready, 1)
                dve.tensor_tensor(mean_gap[:], even[:, :, 1], odd[:, :, 1], ALU.subtract).then_inc(halves_ready, 1)
                dve.tensor_tensor(square_sum[:], even[:, :, 2], odd[:, :, 2], ALU.add).then_inc(halves_ready, 1)
                dve.wait_ge(halves_ready, 3 * b + 3)
                dve.tensor_scalar(mean[:], mean_sum[:], 0.5, None, ALU.mult).then_inc(moments_ready, 1)
                dve.tensor_tensor(gap_square[:], mean_gap[:], mean_gap[:], ALU.mult).then_inc(moments_ready, 1)
                dve.tensor_scalar(inner_var[:], square_sum[:], 1.0 / D, EPS, ALU.mult, ALU.add).then_inc(moments_ready, 1)
                dve.wait_ge(moments_ready, 3 * b + 3)
                dve.scalar_tensor_tensor(var_eps[:], gap_square[:], 0.25, inner_var[:], ALU.mult, ALU.add).then_inc(var_eps_ready, 1)
                dve.wait_ge(rstd_ready, b + 1)
                for t in range(TT):
                    dve.tensor_scalar(xn[:, t], x_tok[:, t], mean[:, t:t + 1], rstd[:, t:t + 1],
                                      ALU.subtract, ALU.mult).then_inc(xn_ready, 1)

            def lo_part(out, psum, b_col, hi):
                dve.scalar_tensor_tensor(out, psum, b_col, hi.bitcast(F32), ALU.add, ALU.subtract).then_inc(lo_out, 1)

            def batch(b, last):
                dve.wait_ge(k_stored, 32 * b + 32)
                for m in range(MT):
                    dve.wait_ge(hi_out, 2 * MT * b + m + 1)
                    lo_part(kst_lo[:, m], proj[:, m], bias[:, 1, m:m + 1], kst_hi[:, m])
                for k in range(KT):
                    dve.wait_ge(xn_hi_ready, KT * b + k + 1)
                    dve.tensor_tensor(xn_lo[:, k], turn[:, k], xn_hi[:, k].bitcast(F32), ALU.subtract).then_inc(xn_lo_ready, 1)
                dve.wait_ge(v_stored, 16 * b + 16)
                for t in range(TT):
                    dve.wait_ge(projected, 3 * MT * b + MT + t + 1)
                    dve.tensor_copy(vst[:, t], proj[:, t]).then_inc(v_out, 1)
                if not last:
                    split_ctx(b + 1)
                    norm(b + 1)
                dve.wait_ge(q_stored, 32 * b + 32)
                for m in range(MT):
                    dve.wait_ge(hi_out, 2 * MT * b + MT + m + 1)
                    lo_part(qst_lo[:, m], proj[:, m], bias[:, 0, m:m + 1], qst_hi[:, m])

            split_ctx(0)
            norm(0)
            with dve.Fori(0, B - 1) as b:
                batch(b, False)
            batch(B - 1, True)

        @block.tensor
        def _(pe):
            def product(out, left, right):
                for k in range(KT):
                    (lh, ll), (rh, rl) = left(k), right(k)
                    pe.matmul(out, lh, rh, start=(k == 0), stop=False)
                    pe.matmul(out, ll, rh, start=False, stop=False)
                    last = pe.matmul(out, lh, rl, start=False, stop=(k == KT - 1))
                last.then_inc(projected, 1)

            def weight(i, m):
                return lambda k: (w_hi[:, i, k, m * P:m * P + P], w_lo[:, i, k, m * P:m * P + P])

            pe.wait_ge(w_lo_ready, 3)

            def batch(b):
                pe.wait_ge(ctx_lo_ready, b + 1)
                for m in range(MT):
                    if not isinstance(b, int) or b > 0:
                        pe.wait_ge(lo_out, 2 * MT * b - MT + m + 1)
                    product(proj[:, m], weight(WK, m), lambda k: (ctx_hi[:, k], ctx_lo[:, k]))
                pe.wait_ge(xn_ready, TT * b + TT)
                for k in range(KT):
                    for t in range(TT):
                        last = pe.transpose(turn[:, k, t * P:t * P + P], xn[:, t, k * P:k * P + P], ident[:])
                    last.then_inc(turned, 1)
                for t in range(TT):
                    pe.wait_ge(lo_out, 2 * MT * b + t + 1)
                    product(proj[:, t], lambda k, t=t: (ctx_hi[:, k, t * P:t * P + P], ctx_lo[:, k, t * P:t * P + P]),
                            lambda k: (w_hi[:, WV, k], w_lo[:, WV, k]))
                pe.wait_ge(xn_lo_ready, KT * b + KT)
                for m in range(MT):
                    pe.wait_ge(v_out, TT * b + m + 1)
                    product(proj[:, m], weight(WQ, m), lambda k: (xn_hi[:, k], xn_lo[:, k]))

            batch(0)
            with pe.Fori(1, B) as b:
                batch(b)


def attend_and_route(nc, x, q_hi, q_lo, k_hi, k_lo, v_raw, wo_t, bv, bo, gates, gate_w_t, consts, x1_rows, rows, counts,
                     heads=HEADS):
    B, S, D = x.shape
    H = heads
    HD = D // H
    SCALE = HD ** -0.5
    KB = S // P
    TT = S // P
    KT = D // P
    GH = P // HD
    NG = H // GH
    E = gate_w_t.shape[1]
    PR = 8
    SK = 3 * HD
    HALF = H // 2

    with ExitStack() as ctx:
        def sb(name, shape, dt=F32):
            return ctx.enter_context(nc.sbuf_tensor(name, shape, dt))

        def sem(name):
            return ctx.enter_context(nc.semaphore(name))

        wo_raw = sb("wo_raw", [P, KT, D])
        wo_hi = sb("wo_hi", [P, KT, D], F32R)
        wo_lo = sb("wo_lo", [P, KT, D], F32R)
        gw = sb("gw", [P, KT, E])
        cst = sb("cst", [P, consts.shape[1]])
        ident = cst[:, 0:P]
        tri_f = cst[:, P:2 * P]
        rev = cst[:, 2 * P:2 * P + TT * E].rearrange("p (t e) -> p t e", e=E)
        tri = sb("tri", [P, P], BF16)
        ones_bf = sb("ones_bf", [P, P], BF16)
        gate_raw = sb("gate_raw", [P, 2])
        gate = sb("gate", [P, 2])
        bv_sb = sb("bv_sb", [P, KT])
        bv_wide = sb("bv_wide", [P, KT, P])
        bo_sb = sb("bo_sb", [1, D])
        ones_f = sb("ones_f", [P, P])
        gated_bias = sb("gated_bias", [P, D])
        zero_row = sb("zero_row", [P, 2 * D])

        qst = sb("qst", [P, H, S], F32R)
        kst = sb("kst", [P, H, S], F32R)
        v_in = [sb(f"v_in_{i}", [P, KB, HALF * HD]) for i in range(2)]
        v_sb = [sb(f"v_{i}", [P, KB, HALF, 2 * HD]) for i in range(2)]
        m_cols = sb("m_cols", [P, 2, KB])
        m_row = sb("m_row", [KB, 2, P], F32R)
        p_exp = sb("p_exp", [P, PR, S])
        o_raw = sb("o_raw", [P, 2, S])
        sums = sb("sums", [P, 2, S])
        recip = sb("recip", [P, S])
        o_t = sb("o_t", [P, S])
        ot_hi = sb("ot_hi", [P, NG, S], F32R)
        ot_lo = sb("ot_lo", [P, NG, S], F32R)
        x_res = sb("x_res", [P, TT, D])
        x1 = sb("x1", [P, TT, D])
        stats = sb("stats2", [P, TT, 6])
        small = sb("small", [P, 8, TT])
        neg_half = sb("neg_half2", [P, TT])
        xr = sb("xr", [P, TT, RW])
        x2t = sb("x2t", [P, KT, S])
        logits_t = sb("logits_t", [E, S])
        rt = sb("rt", [P, 12, TT, E])
        r4 = sb("r4", [P, 10, TT])
        mask = sb("mask", [P, TT, E], BF16)
        tok_id = sb("tok_id", [P, TT])
        carry = sb("carry", [P, E])
        slot_u = sb("slot_u", [P, 2, TT], U32)

        def ps(name, shape):
            return ctx.enter_context(nc.psum_tensor(name, shape, F32))

        smax_ps = ps("smax_ps", [P, 2, S])
        st_ps = ps("st_ps", [P, 2, S])
        pv_ps = ps("pv_ps", [P, 2, S])
        work_ps = ps("work_ps", [P, S])
        turn_ps = ps("turn_ps", [P, S])

        const_loaded = sem("const_loaded")
        const_ready = sem("const_ready")
        bias_ps_ready = sem("bias_ps_ready")
        smax_done = sem("smax_done")
        max_done = sem("max_done")
        m_turned = sem("m_turned")
        m_row_ready = sem("m_row_ready")
        st_done = sem("st_done")
        exp_done = sem("exp_done")
        p_used = sem("p_used")
        o_out = sem("o_out")
        recip_done = sem("recip_done")
        o_norm_ready = sem("o_norm_ready")
        ot_hi_ready = sem("ot_hi_ready")
        ot_lo_ready = sem("ot_lo_ready")
        x_res_loaded = sem("x_res_loaded")
        x_biased = sem("x_biased")
        o_projected = sem("o_projected")
        x1_ready = sem("x1_ready")
        x1_stored = sem("x1_stored")
        stats2_ready = sem("stats2_ready")
        ln_step = sem("ln_step")
        var_eps2_ready = sem("var_eps2_ready")
        rstd2_ready = sem("rstd2_ready")
        xn2_ready = sem("xn2_ready")
        xn2_turned = sem("xn2_turned")
        x2t_ready = sem("x2t_ready")
        gated = sem("gated")
        logits_t_ready = sem("logits_t_ready")
        logits_turned = sem("logits_turned")
        route_step = sem("route_step")
        shifted_ready = sem("shifted_ready")
        exp_gate_ready = sem("exp_gate_ready")
        mask_ready = sem("mask_ready")
        ranked = sem("ranked")
        slots_ready = sem("slots_ready")
        rows_sent = sem("rows_sent")
        rows_stored = sem("rows_stored")
        pads_stored = sem("pads_stored")
        counts_stored = sem("counts_stored")
        const_set = sem("const_set")
        gate_ready = sem("gate_ready")
        bias_ready = sem("bias_ready")
        stack_loaded = [sem(f"stack_loaded_{g}") for g in range(NG)]
        v_loaded = [sem(f"v_loaded_{i}") for i in range(2)]
        v_ready = [sem(f"v_ready_{i}") for i in range(2)]
        m_row_moved = [sem(f"m_row_moved_{i}") for i in range(2)]

        def at_least(eng, semaphore, value):
            if not (isinstance(value, int) and value <= 0):
                eng.wait_ge(semaphore, value)

        def f32(ap):
            return ap.bitcast(F32)

        def head_exists(b, h):
            if isinstance(b, int):
                return 0 <= H * b + h < H * B
            return True

        def group_exists(b, n):
            return not isinstance(b, int) or 0 <= NG * b + n < NG * B

        block = ctx.enter_context(nc.Block())

        def run(eng, slot):
            for b in range(2):
                for h in range(H):
                    slot(b, h)
            with eng.Fori(2, B) as b:
                for h in range(H):
                    slot(b, h)
            for h in range(H):
                slot(B, h)

        @block.sync
        def _(sp):
            for dst, src in ((wo_raw[:], wo_t.rearrange("(k p) n -> p k n", p=P)),
                             (gw[:], gate_w_t.rearrange("(k p) e -> p k e", p=P)),
                             (cst[:], consts), (gate_raw[:], gates), (bv_sb[:], bv), (bo_sb[:], bo)):
                sp.dma_start(dst, src).then_inc(const_loaded, 16)

            def load_stacks(b, g):
                hs = slice(GH * g, GH * g + GH)
                for dst, parts in ((qst, (q_hi, q_hi, q_lo)), (kst, (k_hi, k_lo, k_hi))):
                    for i, part in enumerate(parts):
                        src = part[b, g * P:g * P + P, :].rearrange("(h r) s -> r h s", r=HD)
                        sp.dma_start(f32(dst[HD * i:HD * i + HD, hs, :]), src).then_inc(stack_loaded[g], 16)

            def load_v(b, i):
                src = v_raw[b].rearrange("(k p) d -> p k d", p=P)[:, :, i * HALF * HD:(i + 1) * HALF * HD]
                sp.dma_start(v_in[i][:], src).then_inc(v_loaded[i], 16)

            for g in range(NG):
                load_stacks(0, g)
            load_v(0, 0)
            sp.wait_ge(const_set, 1)
            sp.dma_start(x1_rows[B * S:B * S + 2 * P, :].rearrange("(p j) d -> p (j d)", j=2), zero_row[:]).then_inc(pads_stored, 16)

            def slot(b, h, prefetch=True):
                first, tail = isinstance(b, int) and b == 0, isinstance(b, int) and b == B
                u, c = H * b + h, b - 1
                if h == 0 and not first:
                    at_least(sp, x1_ready, TT * c)
                    sp.dma_start(x_res[:], x[c].rearrange("(t p) d -> p t d", p=P)).then_inc(x_res_loaded, 16)
                if head_exists(b, h - 1):
                    sp.wait_ge(m_row_ready, u)
                    hh = (h - 1) % H
                    sp.dma_start(f32(qst[SK:SK + 1, hh, :]), f32(m_row[:, hh % 2, :])).then_inc(m_row_moved[hh % 2], 16)
                if not tail and not first and h == 1:
                    sp.wait_ge(st_done, KB * H * b)
                    load_stacks(b, NG - 1)
                if not tail and h == 3:
                    at_least(sp, v_ready[1], b)
                    load_v(b, 1)
                if h in (5, 9, 13) and not tail and prefetch:
                    g = (h - 5) // 4
                    sp.wait_ge(st_done, KB * (H * b + GH * g + GH))
                    load_stacks(b + 1, g)
                if h == 8 and not first:
                    sp.wait_ge(x1_ready, TT * b)
                    sp.dma_start(x1_rows[bass.ds(c * S, S), :].rearrange("(t p) d -> p t d", p=P), x1[:]).then_inc(x1_stored, 16)
                if h == 11 and not tail and prefetch:
                    sp.wait_ge(v_ready[0], b + 1)
                    load_v(b + 1, 0)

            for b in range(2):
                for h in range(H):
                    slot(b, h)
            with sp.Fori(2, B - 1) as b:
                for h in range(H):
                    slot(b, h)
            for h in range(H):
                slot(B - 1, h, prefetch=False)
            for h in range(H):
                slot(B, h)
            sp.wait_ge(slots_ready, B)
            sp.dma_start(counts, carry[0:1, :]).then_inc(counts_stored, 16)
            sp.wait_ge(counts_stored, 16)
            sp.wait_ge(pads_stored, 16)
            sp.wait_ge(x1_stored, 16 * B)
            sp.wait_ge(rows_stored, 2 * TT * 16 * B)

        @block.gpsimd
        def _(pool):
            pool.memset(neg_half[:], -0.5).then_inc(const_ready, 1)
            pool.memset(zero_row[:], 0.0).then_inc(const_set, 1)
            pool.wait_ge(const_ready, 1)

            def slot(b, h):
                first, tail = isinstance(b, int) and b == 0, isinstance(b, int) and b == B
                c = b - 1
                G = NG * b + h // GH - 1
                if h % GH == 3 and group_exists(b, h // GH - 1):
                    pool.wait_ge(recip_done, KB * (G + 1))
                    at_least(pool, ot_lo_ready, G)
                    pool.tensor_tensor(o_t[:], o_raw[:, (h // GH + 1) % 2, :], recip[:], ALU.mult).then_inc(o_norm_ready, 1)
                if h % GH == 0 and group_exists(b, h // GH - 2):
                    g = (h // GH - 2) % NG
                    pool.wait_ge(ot_hi_ready, NG * b + h // GH - 1)
                    pool.tensor_tensor(ot_lo[:, g, :], o_t[:], f32(ot_hi[:, g, :]), ALU.subtract).then_inc(ot_lo_ready, 1)
                if h == 1 and not first:
                    pool.wait_ge(x_res_loaded, 16 * b)
                    for t in range(TT):
                        pool.tensor_tensor(x_res[:, t, :], x_res[:, t, :], gated_bias[:], ALU.add).then_inc(x_biased, 1)
                if h == 8 and not first:
                    pool.wait_ge(var_eps2_ready, b)
                    pool.tensor_tensor(small[:, 7, :], small[:, 6, :], neg_half[:], ALU.pow).then_inc(rstd2_ready, 1)
                if h == 15 and not first:
                    pool.wait_ge(slots_ready, b)
                    pool.sem_inc(rows_sent, 1)
                    for k in range(2):
                        for t in range(TT):
                            pool.indirect_dma_start(rows, bass.IndirectOffsetOnAxis(slot_u[:, k, t:t + 1], 0), xr[:, t, :], None).then_inc(rows_stored, 16)

            pool.wait_ge(bias_ready, 1)
            run(pool, slot)

        @block.scalar
        def _(act):
            act.wait_ge(const_loaded, 96)
            act.activation(wo_hi[:], wo_raw[:], ACT.Copy).then_inc(gate_ready, 1)
            act.activation(gate[:], gate_raw[:], ACT.Tanh).then_inc(gate_ready, 1)

            def slot(b, h):
                first, tail = isinstance(b, int) and b == 0, isinstance(b, int) and b == B
                u, c = H * b + h, b - 1
                for kb in range(KB):
                    if head_exists(b, h - 2):
                        w = u - 2
                        act.wait_ge(st_done, KB * w + kb + 1)
                        at_least(act, p_used, KB * w + kb + 1 - PR)
                        act.activation(p_exp[:, (KB * ((h - 2) % H) + kb) % PR, :], st_ps[:, kb % 2, :], ACT.Exp,
                                       scale=SCALE).then_inc(exp_done, 1)
                    if kb == 1:
                        if h in (1, 5) and not tail:
                            i = h // 4
                            act.wait_ge(v_loaded[i], 16 * b + 16)
                            at_least(act, p_used, KB * (H * b - HALF * (1 - i)))
                            act.activation(v_sb[i][:, :, :, 0:HD], v_in[i][:].rearrange("p k (h c) -> p k h c", c=HD),
                                           ACT.Copy).then_inc(v_ready[i], 1)
                        if h % GH == 0 and group_exists(b, h // GH - 2):
                            g = (h // GH - 2) % NG
                            act.wait_ge(o_norm_ready, NG * b + h // GH - 1)
                            at_least(act, o_projected, TT * (b - 1) if g >= 2 else TT * b)
                            act.activation(ot_hi[:, g, :], o_t[:], ACT.Copy).then_inc(ot_hi_ready, 1)
                        if not first and h in (10, 11):
                            x2t_copy(b, 2 * (h - 10) + 1)
                    if kb == 3 and not first and h in (9, 10):
                        x2t_copy(b, 2 * (h - 9))
                if head_exists(b, h - 3):
                    y, hy = u - 3, (h - 3) % H
                    j, par = hy % GH, (hy // GH) % 2
                    act.wait_ge(p_used, KB * (y + 1))
                    if j == 0:
                        at_least(act, o_norm_ready, NG * b + (h - 3) // GH - 1)
                    rows_j = slice(HD * j, HD * j + HD)
                    act.activation(o_raw[rows_j, par, :], pv_ps[0:HD, hy % 2, :], ACT.Copy).then_inc(o_out, 1)
                    act.activation(sums[rows_j, par, :], pv_ps[HD:2 * HD, hy % 2, :], ACT.Copy).then_inc(o_out, 1)
                if not first and h == 13:
                    act.wait_ge(shifted_ready, b)
                    act.activation(rt[:, 1], rt[:, 0], ACT.Exp).then_inc(exp_gate_ready, 1)

            def x2t_copy(b, k):
                act.wait_ge(xn2_turned, KT * (b - 1) + k + 1)
                act.activation(x2t[:, k, :], work_ps[:], ACT.Copy).then_inc(x2t_ready, 1)

            run(act, slot)

        @block.vector
        def _(dve):
            dve.wait_ge(gate_ready, 2)
            dve.wait_ge(const_loaded, 96)
            dve.tensor_tensor(wo_lo[:], wo_raw[:], f32(wo_hi[:]), ALU.subtract).then_inc(bias_ps_ready, 1)
            dve.tensor_copy(tri[:], tri_f).then_inc(bias_ps_ready, 1)
            dve.memset(ones_bf[:], 1.0).then_inc(bias_ps_ready, 1)
            dve.memset(ones_f[:], 1.0).then_inc(bias_ps_ready, 1)
            dve.memset(f32(kst[SK:SK + 1, :, :]), 1.0).then_inc(bias_ps_ready, 1)
            for i in range(2):
                dve.memset(v_sb[i][:, :, :, HD:2 * HD], 1.0).then_inc(bias_ps_ready, 1)
            dve.tensor_copy(tok_id[:], cst[:, 2 * P + TT * E:2 * P + TT * E + TT]).then_inc(bias_ps_ready, 1)
            dve.tensor_copy(carry[:], cst[:, 2 * P + TT * E + TT:2 * P + TT * E + TT + E]).then_inc(bias_ps_ready, 1)
            dve.wait_ge(bias_ps_ready, 9)
            for k in range(KT):
                dve.tensor_scalar(bv_wide[:, k, :], ones_f[:], bv_sb[:, k:k + 1], None, ALU.mult).then_inc(bias_ps_ready, 1)
            dve.wait_ge(gated, 1)
            dve.tensor_scalar(gated_bias[:], work_ps[:], gate[:, 0:1], None, ALU.mult).then_inc(bias_ready, 1)

            LN_STEPS = 6
            RT_STEPS = 26

            def slot(b, h):
                first, tail = isinstance(b, int) and b == 0, isinstance(b, int) and b == B
                u, c = H * b + h, b - 1
                for kb in range(KB):
                    if not tail:
                        dve.wait_ge(smax_done, KB * u + kb + 1)
                        if kb == 0:
                            at_least(dve, m_turned, u - 1)
                        dve.tensor_reduce(m_cols[:, h % 2, kb:kb + 1], smax_ps[:, kb % 2, :], AX_X, ALU.max).then_inc(max_done, 1)
                    if kb == 1 and head_exists(b, h - 1):
                        hh = (h - 1) % H
                        dve.wait_ge(m_turned, u)
                        at_least(dve, m_row_moved[hh % 2], 16 * (8 * b + (h - 1) // 2))
                        dve.tensor_scalar(m_row[:, hh % 2, :], turn_ps[0:KB, 0:P], -1.0, None, ALU.mult).then_inc(m_row_ready, 1)
                    if h % GH == 3 and group_exists(b, h // GH - 1):
                        G = NG * b + h // GH - 1
                        if kb == 0:
                            dve.wait_ge(o_out, 2 * GH * (G + 1))
                            at_least(dve, o_norm_ready, G)
                        blk = slice(kb * P, kb * P + P)
                        dve.reciprocal(recip[:, blk], sums[:, (h // GH + 1) % 2, blk]).then_inc(recip_done, 1)
                    if not first:
                        if h == 5 and kb == 3:
                            residual(b, 0)
                        if h == 6 and kb == 1:
                            residual(b, 1)
                        if h == 6 and kb == 3:
                            residual(b, 2)
                        if h == 7 and kb == 1:
                            residual(b, 3)
                        if h == 8 and kb == 0:
                            moments(b)
                        if h == 8 and kb == 2:
                            norm2(b)
                        if h == 12 and kb == 0:
                            dve.wait_ge(gated, b + 1)
                            at_least(dve, logits_turned, c)
                            dve.tensor_copy(logits_t[:], work_ps[0:E, :]).then_inc(logits_t_ready, 1)
                        if h == 13 and kb == 0:
                            route_scores(b)
                        if h == 13 and kb == 3:
                            route_mask(b)
                        if h == 15 and kb == 0:
                            route_slots(b)

            def residual(b, t):
                n = TT * (b - 1) + t + 1
                dve.wait_ge(o_projected, n)
                if t == 0:
                    dve.wait_ge(x_biased, TT * b)
                    at_least(dve, x1_stored, 16 * (b - 1))
                dve.scalar_tensor_tensor(x1[:, t, :], work_ps[:], gate[:, 0:1], x_res[:, t, :], ALU.mult, ALU.add).then_inc(x1_ready, 1)
                dve.wait_ge(x1_ready, n)
                dve.bn_stats(stats[:, t], x1[:, t, :]).then_inc(stats2_ready, 1)

            def moments(b):
                c = b - 1
                dve.wait_ge(stats2_ready, TT * b)
                even, odd = stats[:, :, 0:3], stats[:, :, 3:6]
                dve.tensor_tensor(small[:, 0], even[:, :, 1], odd[:, :, 1], ALU.add).then_inc(ln_step, 1)
                dve.tensor_tensor(small[:, 1], even[:, :, 1], odd[:, :, 1], ALU.subtract).then_inc(ln_step, 1)
                dve.tensor_tensor(small[:, 2], even[:, :, 2], odd[:, :, 2], ALU.add).then_inc(ln_step, 1)
                dve.wait_ge(ln_step, LN_STEPS * c + 3)
                dve.tensor_scalar(small[:, 3], small[:, 0], 0.5, None, ALU.mult).then_inc(ln_step, 1)
                dve.tensor_tensor(small[:, 4], small[:, 1], small[:, 1], ALU.mult).then_inc(ln_step, 1)
                dve.tensor_scalar(small[:, 5], small[:, 2], 1.0 / D, EPS, ALU.mult, ALU.add).then_inc(ln_step, 1)
                dve.wait_ge(ln_step, LN_STEPS * b)
                dve.scalar_tensor_tensor(small[:, 6], small[:, 4], 0.25, small[:, 5], ALU.mult, ALU.add).then_inc(var_eps2_ready, 1)

            def norm2(b):
                dve.wait_ge(rstd2_ready, b)
                at_least(dve, rows_stored, 2 * TT * 16 * (b - 1))
                for t in range(TT):
                    dve.tensor_scalar(xr[:, t, 0:D], x1[:, t, :], small[:, 3, t:t + 1], small[:, 7, t:t + 1],
                                      ALU.subtract, ALU.mult).then_inc(xn2_ready, 1)

            def wide(ap):
                return ap.unsqueeze(2).to_broadcast([P, TT, E])

            def step_of(b):
                n = [0]

                def step(ins):
                    n[0] += 1
                    ins.then_inc(route_step, 1)

                def done():
                    dve.wait_ge(route_step, RT_STEPS * (b - 1) + n[0])
                return step, done, n

            def route_scores(b):
                step, done, n = step_of(b)
                dve.wait_ge(logits_turned, b)
                logits = work_ps[:, 0:TT * E].rearrange("p (t e) -> p t e", e=E)
                step(dve.tensor_reduce(r4[:, 0], logits, AX_X, ALU.max))
                done()
                dve.tensor_tensor(rt[:, 0], logits, wide(r4[:, 0]), ALU.subtract).then_inc(shifted_ready, 1)
                assert n[0] == 1

            def route_mask(b):
                step, done, n = step_of(b)
                n[0] = 1
                dve.wait_ge(exp_gate_ready, b)
                step(dve.tensor_reduce(r4[:, 1], rt[:, 1], AX_X, ALU.add)); done()
                step(dve.reciprocal(r4[:, 2], r4[:, 1])); done()
                step(dve.tensor_tensor(rt[:, 2], rt[:, 1], wide(r4[:, 2]), ALU.mult)); done()
                prob = rt[:, 2]
                step(dve.tensor_reduce(r4[:, 3], prob, AX_X, ALU.max)); done()
                step(dve.tensor_tensor(rt[:, 3], prob, wide(r4[:, 3]), ALU.is_equal)); done()
                step(dve.tensor_tensor(rt[:, 4], rt[:, 3], rev, ALU.mult)); done()
                step(dve.tensor_reduce(r4[:, 4], rt[:, 4], AX_X, ALU.max)); done()
                step(dve.tensor_tensor(rt[:, 5], rt[:, 4], wide(r4[:, 4]), ALU.is_equal)); done()
                step(dve.scalar_tensor_tensor(rt[:, 6], rt[:, 5], -2.0, prob, ALU.mult, ALU.add)); done()
                step(dve.tensor_reduce(r4[:, 5], rt[:, 6], AX_X, ALU.max)); done()
                step(dve.tensor_tensor(rt[:, 7], rt[:, 6], wide(r4[:, 5]), ALU.is_equal)); done()
                step(dve.tensor_tensor(rt[:, 8], rt[:, 7], rev, ALU.mult)); done()
                step(dve.tensor_reduce(r4[:, 6], rt[:, 8], AX_X, ALU.max)); done()
                step(dve.tensor_tensor(rt[:, 9], rt[:, 8], wide(r4[:, 6]), ALU.is_equal)); done()
                step(dve.tensor_tensor(rt[:, 10], rt[:, 5], rt[:, 9], ALU.add)); done()
                dve.tensor_copy(mask[:], rt[:, 10]).then_inc(mask_ready, 1)
                pairs = xr[:, :, D:D + 2 * E].rearrange("p t (e c) -> p t e c", c=2)
                step(dve.scalar_tensor_tensor(pairs[:, :, :, 1], prob, gate[:, 1:2], rt[:, 10], ALU.mult, ALU.mult))
                step(dve.tensor_copy(pairs[:, :, :, 0], wide(tok_id[:])))
                done()
                step(dve.tensor_scalar(tok_id[:], tok_id[:], float(S), None, ALU.add))
                assert n[0] == 19, n

            def route_slots(b):
                step, done, n = step_of(b)
                n[0] = 19
                dve.wait_ge(ranked, b)
                ranks = work_ps[:, 0:TT * E].rearrange("p (t e) -> p t e", e=E)
                spread = carry[:].unsqueeze(1).to_broadcast([P, TT, E])
                step(dve.tensor_tensor(rt[:, 11], ranks, spread, ALU.add)); done()
                step(dve.tensor_tensor(carry[:], carry[:], work_ps[:, TT * E:TT * E + E], ALU.add))
                step(dve.tensor_tensor(rt[:, 3], rt[:, 11], rt[:, 5], ALU.mult))
                step(dve.tensor_tensor(rt[:, 4], rt[:, 11], rt[:, 9], ALU.mult)); done()
                step(dve.tensor_reduce(r4[:, 7], rt[:, 3], AX_X, ALU.add))
                step(dve.tensor_reduce(r4[:, 8], rt[:, 4], AX_X, ALU.add)); done()
                step(dve.tensor_copy(slot_u[:, 0], r4[:, 7])); done()
                dve.tensor_copy(slot_u[:, 1], r4[:, 8]).then_inc(slots_ready, 1)
                assert n[0] == RT_STEPS, n

            run(dve, slot)

        @block.tensor
        def _(pe):
            pe.wait_ge(const_loaded, 96)
            pe.wait_ge(bias_ps_ready, 9 + KT)
            for k in range(KT):
                pe.matmul(work_ps[:], bv_wide[:, k, :], wo_raw[:, k, :], start=(k == 0), stop=False)
            pe.matmul(work_ps[:], ones_f[0:1, :], bo_sb[:], start=False, stop=True).then_inc(gated, 1)

            def slot(b, h):
                first, tail = isinstance(b, int) and b == 0, isinstance(b, int) and b == B
                u, c = H * b + h, b - 1
                for kb in range(KB):
                    blk = slice(kb * P, kb * P + P)
                    if not tail:
                        if kb == 0 and h % GH == 0:
                            pe.wait_ge(stack_loaded[h // GH], 96 * b + 96)
                        at_least(pe, max_done, KB * u + kb - 1)
                        pe.matmul(smax_ps[:, kb % 2, :], qst[0:SK, h, blk], kst[0:SK, h, :], start=True, stop=True).then_inc(smax_done, 1)
                    if head_exists(b, h - 2):
                        hw, w = (h - 2) % H, u - 2
                        if kb == 0:
                            pe.wait_ge(m_row_moved[hw % 2], 16 * (8 * b + (h - 2) // 2 + 1))
                        at_least(pe, exp_done, KB * w + kb - 1)
                        pe.matmul(st_ps[:, kb % 2, :], kst[0:SK + 1, hw, blk], qst[0:SK + 1, hw, :], start=True, stop=True).then_inc(st_done, 1)
                    if kb == 1 and head_exists(b, h - 1):
                        pe.wait_ge(max_done, KB * u)
                        at_least(pe, m_row_ready, u - 1)
                        pe.transpose(turn_ps[0:KB, 0:P], m_cols[:, (h - 1) % 2, :], ident).then_inc(m_turned, 1)
                    if head_exists(b, h - 3):
                        hy, y = (h - 3) % H, u - 3
                        half, hv = hy // HALF, hy % HALF
                        if kb == 0:
                            if hy == 0:
                                pe.wait_ge(v_ready[0], b + 1)
                            if hy == HALF:
                                pe.wait_ge(v_ready[1], b + 1)
                            at_least(pe, o_out, 2 * (y - 1))
                        pe.wait_ge(exp_done, KB * y + kb + 1)
                        last = pe.matmul(pv_ps[0:2 * HD, hy % 2, :], v_sb[half][:, kb, hv, :], p_exp[:, (KB * hy + kb) % PR, :],
                                         start=(kb == 0), stop=(kb == KB - 1))
                        last.then_inc(p_used, 1)
                    if not first:
                        if h in (5, 6) and kb in (1, 3):
                            out_projection(b, 2 * (h - 5) + kb // 2)
                        if h in (9, 10) and kb in (1, 3):
                            turn_x2(b, 2 * (h - 9) + kb // 2)
                        if h == 11 and kb == 3:
                            gate_logits(b)
                        if h == 12 and kb == 3:
                            turn_logits(b)
                        if h == 14 and kb == 3:
                            rank(b)

            def out_projection(b, t):
                if t == 0:
                    pe.wait_ge(ot_lo_ready, NG * b)
                    at_least(pe, slots_ready, b - 1)
                else:
                    pe.wait_ge(x1_ready, TT * (b - 1) + t)
                tok = slice(t * P, t * P + P)
                for g in range(NG):
                    pe.matmul(work_ps[:], ot_hi[:, g, tok], wo_hi[:, g, :], start=(g == 0), stop=False)
                    pe.matmul(work_ps[:], ot_lo[:, g, tok], wo_hi[:, g, :], start=False, stop=False)
                    last = pe.matmul(work_ps[:], ot_hi[:, g, tok], wo_lo[:, g, :], start=False, stop=(g == NG - 1))
                last.then_inc(o_projected, 1)

            def turn_x2(b, k):
                if k == 0:
                    pe.wait_ge(xn2_ready, TT * b)
                else:
                    pe.wait_ge(x2t_ready, KT * (b - 1) + k)
                for t in range(TT):
                    last = pe.transpose(work_ps[:, t * P:t * P + P], xr[:, t, k * P:k * P + P], ident)
                last.then_inc(xn2_turned, 1)

            def gate_logits(b):
                pe.wait_ge(x2t_ready, KT * b)
                for k in range(KT):
                    last = pe.matmul(work_ps[0:E, :], gw[:, k, :], x2t[:, k, :], start=(k == 0), stop=(k == KT - 1))
                last.then_inc(gated, 1)

            def turn_logits(b):
                pe.wait_ge(logits_t_ready, b)
                for t in range(TT):
                    last = pe.matmul(work_ps[:, t * E:t * E + E], logits_t[:, t * P:t * P + P], cst[0:E, 0:E], start=True, stop=True)
                last.then_inc(logits_turned, 1)

            def rank(b):
                pe.wait_ge(mask_ready, b)
                for t in range(TT):
                    out = work_ps[:, t * E:t * E + E]
                    for before in range(t):
                        pe.matmul(out, ones_bf[:], mask[:, before, :], start=(before == 0), stop=False)
                    pe.matmul(out, tri[:], mask[:, t, :], start=(t == 0), stop=True)
                out = work_ps[:, TT * E:TT * E + E]
                for t in range(TT):
                    last = pe.matmul(out, ones_bf[:], mask[:, t, :], start=(t == 0), stop=(t == TT - 1))
                last.then_inc(ranked, 1)

            run(pe, slot)


def run_experts(nc, rows, counts, w1, w3, w2, ident_dram, first_row, pad_ids, out_rows):
    E, D, HID = w1.shape
    CAP = rows.shape[0] // E
    TB = TILE // P
    KT = D // P
    MB = HID // P
    RING = 4
    CH = 4
    MAX_TILES = (CAP - TILE) // TILE
    ALL_TILES = E * MAX_TILES

    with ExitStack() as ctx:
        def sb(name, shape, dt=F32):
            return ctx.enter_context(nc.sbuf_tensor(name, shape, dt))

        def sem(name):
            return ctx.enter_context(nc.semaphore(name))

        def f32(ap):
            return ap.bitcast(F32)

        up_raw = sb("up_raw", [P, 2, KT, HID])
        up_hi = sb("up_hi", [P, 2, KT, HID], F32R)
        up_lo = sb("up_lo", [P, 2, KT, HID], F32R)
        down_raw = sb("down_raw", [P, MB, D])
        down_hi = sb("down_hi", [P, MB, D], F32R)
        down_lo = sb("down_lo", [P, MB, D], F32R)
        ident = sb("ident_m", [P, P])
        xg = sb("xg", [P, TB, D])
        id_weight = sb("id_weight", [P, TB, 2])
        id_u = sb("id_u", [P, TB], U32)
        xt_hi = sb("xt_hi", [P, KT, TILE], F32R)
        xt_lo = sb("xt_lo", [P, KT, TILE], F32R)
        gated_half = sb("gated_half", [P, 2, TILE])
        h_raw = sb("h_raw", [P, MB, TILE])
        h_hi = sb("h_hi", [P, MB, TILE], F32R)
        h_lo = sb("h_lo", [P, MB, TILE], F32R)
        y = sb("y", [P, TB, D])
        counts_f = sb("counts_f", [1, E])
        first_row_sb = sb("first_row_sb", [1, E])
        pad_ids_sb = sb("pad_ids_sb", [P, TB])
        count_step = sb("count_step", [1, 2, E])
        row_end = sb("row_end", [1, E], I32)
        tiles_i = sb("tiles_i", [1, 2, E], I32)
        tiles = sb("tiles", [1, E], I32)
        pad = sb("pad", [P, TB, RW])
        up_ps = ctx.enter_context(nc.psum_tensor("up_ps", [P, RING, 2, TILE], F32))
        turn_ps = ctx.enter_context(nc.psum_tensor("turn_m_ps", [P, KT, TILE], F32))
        down_ps = ctx.enter_context(nc.psum_tensor("down_ps", [P, TB, D], F32))

        setup_loaded = sem("setup_loaded")
        count_steps = sem("count_steps")
        pad_zeroed = sem("pad_zeroed")
        pads_written = sem("pads_written")
        weights_loaded = sem("weights_loaded")
        up_hi_ready = sem("up_hi_ready")
        up_lo_ready = sem("up_lo_ready")
        down_hi_ready = sem("down_hi_ready")
        down_lo_ready = sem("down_lo_ready")
        xg_loaded = sem("xg_loaded")
        id_loaded = sem("id_loaded")
        turned = sem("turned_m")
        xt_hi_ready = sem("xt_hi_ready")
        xt_lo_ready = sem("xt_lo_ready")
        up_done = sem("up_done")
        silu_ready = sem("silu_ready")
        h_made = sem("h_made")
        h_hi_ready = sem("h_hi_ready")
        h_lo_ready = sem("h_lo_ready")
        down_done = sem("down_done")
        y_made = sem("y_made")
        y_seen = sem("y_seen")
        scattered = sem("scattered")
        y_sent = sem("y_sent")
        UP_PARTS = 2 * CH

        block = ctx.enter_context(nc.Block())

        def tile_loops(eng, body, expert=None, peel_last=False):
            r = eng.alloc_register("tiles_before")
            eng.reg_mov(r, 0)

            def one(e):
                if expert:
                    expert(e, eng.snap(r, min_val=0, max_val=ALL_TILES))
                before = eng.snap(r, min_val=0, max_val=ALL_TILES)
                n = eng.value_load(tiles[0:1, bass.ds(e, 1)], min_val=1, max_val=MAX_TILES)
                with eng.Fori(0, n) as i:
                    body(e, i, before + i)
                eng.reg_add(r, r, n)

            with eng.Fori(0, E - 1 if peel_last else E) as e:
                one(e)
            if peel_last:
                one(E - 1)
            return eng.snap(r, min_val=1, max_val=ALL_TILES)

        def load_weights(eng, e):
            for i, w in enumerate((w1, w3)):
                eng.dma_start(up_raw[:, i], w[e].rearrange("(k p) n -> p k n", p=P)).then_inc(weights_loaded, 16)
            eng.dma_start(down_raw[:], w2[e].rearrange("(m p) n -> p m n", p=P)).then_inc(weights_loaded, 16)

        @block.sync
        def _(sp):
            for dst, src in ((counts_f, counts), (first_row_sb, first_row), (pad_ids_sb, pad_ids), (ident, ident_dram)):
                sp.dma_start(dst[:], src).then_inc(setup_loaded, 16)
            sp.wait_ge(count_steps, 7)
            for e in range(E):
                end = sp.value_load(row_end[0:1, e:e + 1], min_val=e * CAP, max_val=(e + 1) * CAP - TILE)
                sp.dma_start(rows[bass.ds(end, TILE), :].rearrange("(t p) d -> p t d", p=P), pad[:]).then_inc(pads_written, 16)
            sp.wait_ge(pads_written, 16 * E)

            def tile(e, i, f):
                start = e * CAP + i * TILE
                sp.wait_ge(turned, f * 2 + 2)
                sp.dma_start(xg[:], rows[bass.ds(start, TILE), 0:D].rearrange("(t p) d -> p t d", p=P)).then_inc(xg_loaded, 16)
                sp.wait_ge(y_made, f * TB + TB)
                sp.dma_start(id_weight[:], rows[bass.ds(start, TILE), bass.ds(e * 2 + D, 2)].rearrange("(t p) c -> p t c", p=P)).then_inc(id_loaded, 16)

            total = tile_loops(sp, tile)
            sp.wait_ge(turned, total * 2 + 2)
            sp.dma_start(xg[:], rows[0:TILE, 0:D].rearrange("(t p) d -> p t d", p=P)).then_inc(xg_loaded, 16)

        @block.gpsimd
        def _(pool):
            pool.memset(pad[:], 0.0).then_inc(pad_zeroed, 1)
            pool.sem_inc(y_sent, 1)
            pool.wait_ge(count_steps, 7)

            def tile(e, i, f):
                for t in range(TB):
                    pool.wait_ge(y_made, f * TB + (TB + t + 1))
                    pool.sem_inc(y_seen, 1)
                    pool.indirect_dma_start(out_rows, bass.IndirectOffsetOnAxis(id_u[:, t:t + 1], 0), y[:, t, :], None,
                                            compute_op=ALU.add).then_inc(scattered, 16)
                pool.wait_ge(scattered, f * 32 + 32)
                pool.sem_inc(y_sent, 1)

            tile_loops(pool, tile)

        @block.scalar
        def _(act):
            load_weights(act, 0)
            act.wait_ge(count_steps, 7)

            def turn_hi(f):
                for j in range(2):
                    act.wait_ge(turned, f * 2 + (2 + j + 1))
                    act.activation(xt_hi[:, 2 * j:2 * j + 2, :], turn_ps[:, 2 * j:2 * j + 2, :], ACT.Copy).then_inc(xt_hi_ready, 1)

            def expert(e, f):
                act.wait_ge(weights_loaded, e * 48 + 48)
                act.wait_ge(turned, f * 2 + 4)
                W = HID // CH
                for c in range(CH):
                    for i in range(2):
                        cols = slice(c * W, c * W + W)
                        act.activation(up_hi[:, i, :, cols], up_raw[:, i, :, cols], ACT.Copy).then_inc(up_hi_ready, 1)
                act.wait_ge(down_done, f * TB + TB)
                for c in range(CH):
                    ms = slice(c * MB // CH, (c + 1) * MB // CH)
                    act.activation(down_hi[:, ms, :], down_raw[:, ms, :], ACT.Copy).then_inc(down_hi_ready, 1)
                if not isinstance(e, int):
                    act.wait_ge(down_lo_ready, e * CH + CH)
                    load_weights(act, e + 1)

            def tile(e, i, f):
                def hi(m):
                    act.wait_ge(h_made, f * MB + (RING + m + 1))
                    if m == 0:
                        act.wait_ge(down_done, f * TB + TB)
                    act.activation(h_hi[:, m, :], h_raw[:, m, :], ACT.Copy).then_inc(h_hi_ready, 1)

                for m in range(MB):
                    act.wait_ge(up_done, f * MB + (m + 1))
                    act.wait_ge(h_made, f * MB + (RING + m - 1))
                    act.activation(gated_half[:, m % 2, :], up_ps[:, m % RING, 0, :], ACT.Silu).then_inc(silu_ready, 1)
                    if m:
                        hi(m - 1)
                hi(MB - 1)
                turn_hi(f + 1)

            turn_hi(0)
            tile_loops(act, tile, expert, peel_last=True)

        @block.vector
        def _(dve):
            dve.sem_inc(h_made, RING)
            dve.sem_inc(y_made, TB)
            dve.wait_ge(setup_loaded, 64)
            dve.tensor_tensor(count_step[:, 0], counts_f[:], first_row_sb[:], ALU.subtract).then_inc(count_steps, 1)
            dve.tensor_copy(row_end[:], counts_f[:]).then_inc(count_steps, 1)
            dve.wait_ge(pad_zeroed, 1)
            pairs = pad[:, :, D:D + 2 * E].rearrange("p t (e c) -> p t e c", c=2)
            dve.tensor_copy(pairs[:, :, :, 0], pad_ids_sb[:].unsqueeze(2).to_broadcast([P, TB, E])).then_inc(count_steps, 1)
            dve.wait_ge(count_steps, 3)
            dve.tensor_scalar(count_step[:, 1], count_step[:, 0], float(TILE - 1), None, ALU.add).then_inc(count_steps, 1)
            dve.wait_ge(count_steps, 4)
            dve.tensor_copy(tiles_i[:, 0], count_step[:, 1]).then_inc(count_steps, 1)
            dve.wait_ge(count_steps, 5)
            dve.tensor_scalar(tiles_i[:, 1], tiles_i[:, 0], TILE.bit_length() - 1, None, ALU.arith_shift_right).then_inc(count_steps, 1)
            dve.wait_ge(count_steps, 6)
            dve.tensor_scalar(tiles[:], tiles_i[:, 1], 1, None, ALU.max).then_inc(count_steps, 1)
            dve.wait_ge(count_steps, 7)

            def turn_lo(f):
                for j in range(2):
                    dve.wait_ge(xt_hi_ready, f * 2 + (j + 1))
                    dve.tensor_tensor(xt_lo[:, 2 * j:2 * j + 2, :], turn_ps[:, 2 * j:2 * j + 2, :],
                                      f32(xt_hi[:, 2 * j:2 * j + 2, :]), ALU.subtract).then_inc(xt_lo_ready, 1)

            def expert(e, f):
                W = HID // CH
                for c in range(CH):
                    for i in range(2):
                        cols = slice(c * W, c * W + W)
                        dve.wait_ge(up_hi_ready, e * UP_PARTS + (2 * c + i + 1))
                        dve.tensor_tensor(up_lo[:, i, :, cols], up_raw[:, i, :, cols], f32(up_hi[:, i, :, cols]), ALU.subtract).then_inc(up_lo_ready, 1)
                for c in range(CH):
                    ms = slice(c * MB // CH, (c + 1) * MB // CH)
                    dve.wait_ge(down_hi_ready, e * CH + (c + 1))
                    dve.tensor_tensor(down_lo[:, ms, :], down_raw[:, ms, :], f32(down_hi[:, ms, :]), ALU.subtract).then_inc(down_lo_ready, 1)

            def weigh(f):
                dve.wait_ge(id_loaded, f * 16 + 16)
                dve.wait_ge(y_sent, f + 1)
                dve.tensor_copy(id_u[:], id_weight[:, :, 0])
                for t in range(TB):
                    dve.wait_ge(down_done, f * TB + (TB + t + 1))
                    dve.tensor_scalar(y[:, t, :], down_ps[:, t, :], id_weight[:, t, 1:2], None, ALU.mult).then_inc(y_made, 1)

            def tile(e, i, f):
                def lo(m):
                    dve.wait_ge(h_hi_ready, f * MB + (m + 1))
                    dve.tensor_tensor(h_lo[:, m, :], h_raw[:, m, :], f32(h_hi[:, m, :]), ALU.subtract).then_inc(h_lo_ready, 1)

                for m in range(MB):
                    dve.wait_ge(silu_ready, f * MB + (m + 1))
                    dve.tensor_tensor(h_raw[:, m, :], gated_half[:, m % 2, :], up_ps[:, m % RING, 1, :], ALU.mult).then_inc(h_made, 1)
                    if m:
                        lo(m - 1)
                lo(MB - 1)
                turn_lo(f + 1)
                weigh(f)

            turn_lo(0)
            tile_loops(dve, tile, expert)

        @block.tensor
        def _(pe):
            pe.sem_inc(turned, 2)
            pe.sem_inc(down_done, TB)
            pe.wait_ge(count_steps, 7)
            pe.wait_ge(setup_loaded, 64)

            def turn(f):
                pe.wait_ge(xg_loaded, f * 16 + 16)
                for k in range(KT):
                    for t in range(TB):
                        last = pe.transpose(turn_ps[:, k, t * P:t * P + P], xg[:, t, k * P:k * P + P], ident[:])
                    if k % 2:
                        last.then_inc(turned, 1)

            def tile(e, i, f):
                pe.wait_ge(xt_lo_ready, f * 2 + 2)
                for m in range(MB):
                    if m % (MB // CH) == 0:
                        pe.wait_ge(up_lo_ready, e * UP_PARTS + (2 * (m * CH // MB) + 2))
                    pe.wait_ge(h_made, f * MB + (m + 1))
                    cols = slice(m * P, m * P + P)
                    for w in range(2):
                        out = up_ps[:, m % RING, w, :]
                        for k in range(KT):
                            pe.matmul(out, up_hi[:, w, k, cols], xt_hi[:, k, :], start=(k == 0), stop=False)
                            pe.matmul(out, up_lo[:, w, k, cols], xt_hi[:, k, :], start=False, stop=False)
                            last = pe.matmul(out, up_hi[:, w, k, cols], xt_lo[:, k, :], start=False, stop=(k == KT - 1))
                    last.then_inc(up_done, 1)
                turn(f + 1)
                for t in range(TB):
                    pe.wait_ge(y_made, f * TB + (t + 1))
                    tok = slice(t * P, t * P + P)
                    for m in range(MB):
                        if t == 0:
                            if m % (MB // CH) == 0:
                                pe.wait_ge(down_lo_ready, e * CH + (m * CH // MB + 1))
                            pe.wait_ge(h_lo_ready, f * MB + (m + 1))
                        pe.matmul(down_ps[:, t, :], h_hi[:, m, tok], down_hi[:, m, :], start=(m == 0), stop=False)
                        pe.matmul(down_ps[:, t, :], h_lo[:, m, tok], down_hi[:, m, :], start=False, stop=False)
                        last = pe.matmul(down_ps[:, t, :], h_hi[:, m, tok], down_lo[:, m, :], start=False, stop=(m == MB - 1))
                    last.then_inc(down_done, 1)

            turn(0)
            tile_loops(pe, tile)


def build(nc, x, ctx_t, wq_t, wk_t, wv_t, wo_t, bq, bk, bv, bo, gates, gate_w_t, w1, w3, w2, ident, consts, first_row, pad_ids, out_rows):
    B, S, D = x.shape
    E = w1.shape[0]
    capacity = B * S + TILE
    q_hi, q_lo, k_hi, k_lo = [nc.dram_tensor(n, [B, D, S], F32).ap() for n in ("q_hi", "q_lo", "k_hi", "k_lo")]
    v_raw = nc.dram_tensor("v_raw", [B, S, D], F32).ap()
    rows = nc.dram_tensor("rows", [E * capacity, RW], F32).ap()
    counts = nc.dram_tensor("counts", [1, E], F32).ap()
    project_qkv(nc, x, ctx_t, wq_t, wk_t, wv_t, bq, bk, ident, q_hi, q_lo, k_hi, k_lo, v_raw)
    attend_and_route(nc, x, q_hi, q_lo, k_hi, k_lo, v_raw, wo_t, bv, bo, gates, gate_w_t, consts, out_rows, rows, counts)
    run_experts(nc, rows, counts, w1, w3, w2, ident, first_row, pad_ids, out_rows)


def kernel(x, ctx_1024, g_xattn, g_ffn, L0_xattn_w_q, L0_xattn_b_q, L0_xattn_w_k, L0_xattn_b_k, L0_xattn_w_v,
           L0_xattn_b_v, L0_xattn_w_o, L0_xattn_b_o, L0_ffn_gate_w, L0_ffn_w1, L0_ffn_w2, L0_ffn_w3):
    import numpy as np
    import concourse.bacc as bacc
    from concourse.bass_utils import run_bass_kernel_spmd

    B, S, D = x.shape
    E = L0_ffn_w1.shape[0]
    TT = S // P
    capacity = B * S + TILE

    def columns(b):
        return np.asarray(b).reshape(D // P, P).T

    eye = np.eye(P, dtype=np.float32)
    token = np.arange(P, dtype=np.float32)[:, None] + P * np.arange(TT, dtype=np.float32)
    first_row = capacity * np.arange(E, dtype=np.float32)[None, :]
    consts = np.concatenate([
        eye,
        np.triu(np.ones((P, P), np.float32), 1),
        np.broadcast_to(np.tile(E - np.arange(E, dtype=np.float32), TT), (P, TT * E)),
        token,
        np.broadcast_to(first_row, (P, E)),
    ], axis=1)
    arrays = dict(
        x=x, ctx_t=np.asarray(ctx_1024).transpose(0, 2, 1),
        wq_t=np.asarray(L0_xattn_w_q).T, wk_t=np.asarray(L0_xattn_w_k).T, wv_t=np.asarray(L0_xattn_w_v).T,
        wo_t=np.asarray(L0_xattn_w_o).T,
        bq=columns(L0_xattn_b_q), bk=columns(L0_xattn_b_k), bv=columns(L0_xattn_b_v),
        bo=np.asarray(L0_xattn_b_o)[None, :],
        gates=np.broadcast_to(np.concatenate([np.asarray(g_xattn), np.asarray(g_ffn)])[None, :], (P, 2)),
        gate_w_t=np.asarray(L0_ffn_gate_w).T, w1=L0_ffn_w1, w3=L0_ffn_w3, w2=L0_ffn_w2,
        ident=eye, consts=consts, first_row=first_row,
        pad_ids=B * S + token[:, 0:TILE // P],
    )
    nc = bacc.Bacc("TRN2", target_bir_lowering=False, num_devices=1)
    ins, args = {}, []
    for name, a in arrays.items():
        a = np.ascontiguousarray(a)
        ins[f"in_{name}_dram"] = a
        args.append(nc.dram_tensor(f"in_{name}_dram", a.shape, mybir.dt.from_np(a.dtype), kind="ExternalInput").ap())
    out = nc.dram_tensor("out_0_dram", (B * S + TILE, D), F32, kind="ExternalOutput").ap()
    build(nc, *args, out)
    got = run_bass_kernel_spmd(nc, [ins], core_ids=[0]).results[0]["out_0_dram"]
    return got[:B * S].reshape(B, S, D)
```

```python
from contextlib import ExitStack

import concourse.bass as bass
from concourse import mybir

F32 = mybir.dt.float32
F32R = mybir.dt.float32r
BF16 = mybir.dt.bfloat16
I32 = mybir.dt.int32
U32 = mybir.dt.uint32
ALU = mybir.AluOpType
ACT = mybir.ActivationFunctionType
AX_X = mybir.AxisListType.X

P = 128
EPS = 1e-5
RW = 528
TILE = 256
HEADS = 16


def project_qkv(nc, x, ctx_t, wq_t, wk_t, wv_t, bq, bk, ident_dram, q_parts, k_parts, v_raw):
    B, S, D = x.shape
    KT = D // P
    MT = D // P
    TT = S // P
    HD = q_parts.shape[3]
    GH = P // HD
    SENT = 2 * GH * 16

    with ExitStack() as ctx:
        def sb(name, shape, dt=F32):
            return ctx.enter_context(nc.sbuf_tensor(name, shape, dt))

        def sem(name):
            return ctx.enter_context(nc.semaphore(name))

        w_raw = sb("w_raw", [P, 3, KT, D])
        w_hi = sb("w_hi", [P, 3, KT, D], F32R)
        w_lo = sb("w_lo", [P, 3, KT, D], F32R)
        WQ, WK, WV = range(3)
        bias = sb("bias", [P, 2, MT])
        ident = sb("ident_a", [P, P])
        x_tok = sb("x_tok", [P, TT, D])
        xn = sb("xn", [P, TT, D])
        stats = sb("stats", [P, TT, 6])
        mean_sum = sb("mean_sum", [P, TT])
        mean_gap = sb("mean_gap", [P, TT])
        square_sum = sb("square_sum", [P, TT])
        mean = sb("mean", [P, TT])
        gap_square = sb("gap_square", [P, TT])
        inner_var = sb("inner_var", [P, TT])
        var_eps = sb("var_eps", [P, TT])
        rstd = sb("rstd", [P, TT])
        neg_half = sb("neg_half", [P, TT])
        ctx_raw = sb("ctx_raw", [P, KT, S])
        ctx_hi = sb("ctx_hi", [P, KT, S], F32R)
        ctx_lo = sb("ctx_lo", [P, KT, S], F32R)
        xn_hi = sb("xn_hi", [P, KT, S], F32R)
        xn_lo = sb("xn_lo", [P, KT, S], F32R)
        kst_hi = sb("kst_hi", [P, MT, S], F32R)
        kst_lo = sb("kst_lo", [P, MT, S], F32R)
        qst_hi = sb("qst_hi", [P, MT, S], F32R)
        qst_lo = sb("qst_lo", [P, MT, S], F32R)
        vst = sb("vst", [P, TT, D])
        proj = ctx.enter_context(nc.psum_tensor("proj", [P, 4, S], F32))
        turn = ctx.enter_context(nc.psum_tensor("turn", [P, KT, S], F32))

        w_loaded = [sem(f"w_loaded_{n}") for n in "qkv"]
        small_loaded = sem("small_loaded")
        w_hi_ready = sem("w_hi_ready")
        w_lo_ready = sem("w_lo_ready")
        pow_const_ready = sem("pow_const_ready")
        x_loaded = sem("x_loaded")
        ctx_loaded = sem("ctx_loaded")
        stats_ready = sem("stats_ready")
        halves_ready = sem("halves_ready")
        moments_ready = sem("moments_ready")
        var_eps_ready = sem("var_eps_ready")
        rstd_ready = sem("rstd_ready")
        xn_ready = sem("xn_ready")
        ctx_hi_ready = sem("ctx_hi_ready")
        ctx_lo_ready = sem("ctx_lo_ready")
        turned = sem("turned")
        xn_hi_ready = sem("xn_hi_ready")
        xn_lo_ready = sem("xn_lo_ready")
        projected = sem("projected")
        hi_out = sem("hi_out")
        lo_out = sem("lo_out")
        v_out = sem("v_out")
        k_stored = sem("k_stored")
        q_stored = sem("q_stored")
        v_stored = sem("v_stored")

        block = ctx.enter_context(nc.Block())

        @block.sync
        def _(sp):
            def load_weight(i):
                w = (wq_t, wk_t, wv_t)[i]
                sp.dma_start(w_raw[:, i], w.rearrange("(k p) n -> p k n", p=P)).then_inc(w_loaded[i], 16)

            def load_ctx(b):
                sp.dma_start(ctx_raw[:], ctx_t[b].rearrange("(k p) s -> p k s", p=P)).then_inc(ctx_loaded, 16)

            def load_x(b):
                sp.dma_start(x_tok[:], x[b].rearrange("(t p) d -> p t d", p=P)).then_inc(x_loaded, 16)

            def store_heads(parts, b, part, tile, stored):
                heads = parts[b].rearrange("(m g) c r s -> g c r m s", g=GH)
                for g in range(GH):
                    sp.dma_start(heads[g, part], tile[g * HD:g * HD + HD].bitcast(F32)).then_inc(stored, 16)

            def batch(b, last):
                if not last:
                    sp.wait_ge(ctx_hi_ready, b + 1)
                    sp.wait_ge(ctx_lo_ready, b + 1)
                    sp.wait_ge(xn_ready, TT * b + TT)
                    load_ctx(b + 1)
                    load_x(b + 1)
                sp.wait_ge(hi_out, 2 * MT * b + MT)
                store_heads(k_parts, b, 0, kst_hi, k_stored)
                sp.wait_ge(lo_out, 2 * MT * b + MT)
                store_heads(k_parts, b, 1, kst_lo, k_stored)
                sp.wait_ge(v_out, TT * b + TT)
                sp.dma_start(v_raw[b].rearrange("(t p) d -> p t d", p=P), vst[:]).then_inc(v_stored, 16)
                sp.wait_ge(hi_out, 2 * MT * b + 2 * MT)
                store_heads(q_parts, b, 0, qst_hi, q_stored)
                sp.wait_ge(lo_out, 2 * MT * b + 2 * MT)
                store_heads(q_parts, b, 1, qst_lo, q_stored)

            load_weight(WK)
            load_ctx(0)
            for dst, src in ((bias[:, 0], bq), (bias[:, 1], bk), (ident[:], ident_dram)):
                sp.dma_start(dst, src).then_inc(small_loaded, 16)
            load_x(0)
            load_weight(WV)
            load_weight(WQ)
            with sp.Fori(0, B - 1) as b:
                batch(b, False)
            batch(B - 1, True)
            sp.wait_ge(k_stored, SENT * B + SENT)
            sp.wait_ge(q_stored, SENT * B + SENT)
            sp.wait_ge(v_stored, 16 * B + 16)

        @block.gpsimd
        def _(pool):
            pool.memset(neg_half[:], -0.5).then_inc(pow_const_ready, 1)
            pool.wait_ge(pow_const_ready, 1)
            with pool.Fori(0, B) as b:
                pool.wait_ge(var_eps_ready, b + 1)
                pool.tensor_tensor(rstd[:], var_eps[:], neg_half[:], ALU.pow).then_inc(rstd_ready, 1)

        @block.scalar
        def _(act):
            def split_weight(i):
                act.wait_ge(w_loaded[i], 16)
                act.activation(w_hi[:, i], w_raw[:, i], ACT.Copy).then_inc(w_hi_ready, 1)

            act.sem_inc(k_stored, SENT)
            act.sem_inc(q_stored, SENT)
            act.sem_inc(v_stored, 16)

            def split_ctx(b):
                act.wait_ge(ctx_loaded, 16 * b + 16)
                act.activation(ctx_hi[:], ctx_raw[:], ACT.Copy).then_inc(ctx_hi_ready, 1)

            def batch(b, last):
                act.wait_ge(k_stored, SENT * b + SENT)
                for m in range(MT):
                    act.wait_ge(projected, 3 * MT * b + m + 1)
                    act.activation(kst_hi[:, m], proj[:, m], ACT.Identity, bias=bias[:, 1, m:m + 1]).then_inc(hi_out, 1)
                for k in range(KT):
                    act.wait_ge(turned, KT * b + k + 1)
                    act.activation(xn_hi[:, k], turn[:, k], ACT.Copy).then_inc(xn_hi_ready, 1)
                if not last:
                    act.wait_ge(projected, 3 * MT * b + 2 * MT)
                    split_ctx(b + 1)
                act.wait_ge(q_stored, SENT * b + SENT)
                for m in range(MT):
                    act.wait_ge(projected, 3 * MT * b + 2 * MT + m + 1)
                    act.activation(qst_hi[:, m], proj[:, m], ACT.Identity, bias=bias[:, 0, m:m + 1]).then_inc(hi_out, 1)

            split_weight(WK)
            split_ctx(0)
            act.wait_ge(small_loaded, 48)
            split_weight(WV)
            split_weight(WQ)
            with act.Fori(0, B - 1) as b:
                batch(b, False)
            batch(B - 1, True)

        @block.vector
        def _(dve):
            def split_weight(n, i):
                dve.wait_ge(w_hi_ready, n + 1)
                dve.tensor_tensor(w_lo[:, i], w_raw[:, i], w_hi[:, i].bitcast(F32), ALU.subtract).then_inc(w_lo_ready, 1)

            def split_ctx(b):
                dve.wait_ge(ctx_hi_ready, b + 1)
                dve.tensor_tensor(ctx_lo[:], ctx_raw[:], ctx_hi[:].bitcast(F32), ALU.subtract).then_inc(ctx_lo_ready, 1)

            def norm(b):
                dve.wait_ge(x_loaded, 16 * b + 16)
                for t in range(TT):
                    dve.bn_stats(stats[:, t], x_tok[:, t]).then_inc(stats_ready, 1)
                dve.wait_ge(stats_ready, TT * b + TT)
                even, odd = stats[:, :, 0:3], stats[:, :, 3:6]
                dve.tensor_tensor(mean_sum[:], even[:, :, 1], odd[:, :, 1], ALU.add).then_inc(halves_ready, 1)
                dve.tensor_tensor(mean_gap[:], even[:, :, 1], odd[:, :, 1], ALU.subtract).then_inc(halves_ready, 1)
                dve.tensor_tensor(square_sum[:], even[:, :, 2], odd[:, :, 2], ALU.add).then_inc(halves_ready, 1)
                dve.wait_ge(halves_ready, 3 * b + 3)
                dve.tensor_scalar(mean[:], mean_sum[:], 0.5, None, ALU.mult).then_inc(moments_ready, 1)
                dve.tensor_tensor(gap_square[:], mean_gap[:], mean_gap[:], ALU.mult).then_inc(moments_ready, 1)
                dve.tensor_scalar(inner_var[:], square_sum[:], 1.0 / D, EPS, ALU.mult, ALU.add).then_inc(moments_ready, 1)
                dve.wait_ge(moments_ready, 3 * b + 3)
                dve.scalar_tensor_tensor(var_eps[:], gap_square[:], 0.25, inner_var[:], ALU.mult, ALU.add).then_inc(var_eps_ready, 1)
                dve.wait_ge(rstd_ready, b + 1)
                for t in range(TT):
                    dve.tensor_scalar(xn[:, t], x_tok[:, t], mean[:, t:t + 1], rstd[:, t:t + 1],
                                      ALU.subtract, ALU.mult).then_inc(xn_ready, 1)

            def lo_part(out, psum, b_col, hi):
                dve.scalar_tensor_tensor(out, psum, b_col, hi.bitcast(F32), ALU.add, ALU.subtract).then_inc(lo_out, 1)

            def batch(b, last):
                dve.wait_ge(k_stored, SENT * b + SENT)
                for m in range(MT):
                    dve.wait_ge(hi_out, 2 * MT * b + m + 1)
                    lo_part(kst_lo[:, m], proj[:, m], bias[:, 1, m:m + 1], kst_hi[:, m])
                for k in range(KT):
                    dve.wait_ge(xn_hi_ready, KT * b + k + 1)
                    dve.tensor_tensor(xn_lo[:, k], turn[:, k], xn_hi[:, k].bitcast(F32), ALU.subtract).then_inc(xn_lo_ready, 1)
                dve.wait_ge(v_stored, 16 * b + 16)
                for t in range(TT):
                    dve.wait_ge(projected, 3 * MT * b + MT + t + 1)
                    dve.tensor_copy(vst[:, t], proj[:, t]).then_inc(v_out, 1)
                if not last:
                    split_ctx(b + 1)
                    norm(b + 1)
                dve.wait_ge(q_stored, SENT * b + SENT)
                for m in range(MT):
                    dve.wait_ge(hi_out, 2 * MT * b + MT + m + 1)
                    lo_part(qst_lo[:, m], proj[:, m], bias[:, 0, m:m + 1], qst_hi[:, m])

            split_weight(0, WK)
            split_ctx(0)
            dve.wait_ge(small_loaded, 48)
            norm(0)
            split_weight(1, WV)
            split_weight(2, WQ)
            with dve.Fori(0, B - 1) as b:
                batch(b, False)
            batch(B - 1, True)

        @block.tensor
        def _(pe):
            def product(out, left, right):
                for k in range(KT):
                    (lh, ll), (rh, rl) = left(k), right(k)
                    pe.matmul(out, lh, rh, start=(k == 0), stop=False)
                    pe.matmul(out, ll, rh, start=False, stop=False)
                    last = pe.matmul(out, lh, rl, start=False, stop=(k == KT - 1))
                last.then_inc(projected, 1)

            def weight(i, m):
                return lambda k: (w_hi[:, i, k, m * P:m * P + P], w_lo[:, i, k, m * P:m * P + P])

            def batch(b):
                pe.wait_ge(ctx_lo_ready, b + 1)
                if isinstance(b, int):
                    pe.wait_ge(w_lo_ready, 1)
                for m in range(MT):
                    if not isinstance(b, int) or b > 0:
                        pe.wait_ge(lo_out, 2 * MT * b - MT + m + 1)
                    product(proj[:, m], weight(WK, m), lambda k: (ctx_hi[:, k], ctx_lo[:, k]))
                if isinstance(b, int):
                    pe.wait_ge(small_loaded, 48)
                pe.wait_ge(xn_ready, TT * b + TT)
                for k in range(KT):
                    for t in range(TT):
                        last = pe.transpose(turn[:, k, t * P:t * P + P], xn[:, t, k * P:k * P + P], ident[:])
                    last.then_inc(turned, 1)
                if isinstance(b, int):
                    pe.wait_ge(w_lo_ready, 3)
                for t in range(TT):
                    pe.wait_ge(lo_out, 2 * MT * b + t + 1)
                    product(proj[:, t], lambda k, t=t: (ctx_hi[:, k, t * P:t * P + P], ctx_lo[:, k, t * P:t * P + P]),
                            lambda k: (w_hi[:, WV, k], w_lo[:, WV, k]))
                pe.wait_ge(xn_lo_ready, KT * b + KT)
                for m in range(MT):
                    pe.wait_ge(v_out, TT * b + m + 1)
                    product(proj[:, m], weight(WQ, m), lambda k: (xn_hi[:, k], xn_lo[:, k]))

            batch(0)
            with pe.Fori(1, B) as b:
                batch(b)


def attend_and_route(nc, x, q_parts, k_parts, v_raw, wo_t, bv, bo, gates, gate_w_t, consts, x1_rows, rows, counts,
                     heads=HEADS):
    B, S, D = x.shape
    H = heads
    HD = D // H
    SCALE = HD ** -0.5
    KB = S // P
    TT = S // P
    KT = D // P
    GH = P // HD
    NG = H // GH
    E = gate_w_t.shape[1]
    VW = 3 * HD
    DVE_LO = (3,)
    SK = 3 * HD
    HALF = H // 2

    with ExitStack() as ctx:
        def sb(name, shape, dt=F32):
            return ctx.enter_context(nc.sbuf_tensor(name, shape, dt))

        def sem(name):
            return ctx.enter_context(nc.semaphore(name))

        wo_raw = sb("wo_raw", [P, KT, D])
        wo_hi = sb("wo_hi", [P, KT, D], F32R)
        wo_lo = sb("wo_lo", [P, KT, D], F32R)
        gw = sb("gw", [P, KT, E])
        cst = sb("cst", [P, consts.shape[1]])
        ident = cst[:, 0:P]
        tri_f = cst[:, P:2 * P]
        rev = cst[:, 2 * P:2 * P + TT * E].rearrange("p (t e) -> p t e", e=E)
        tri = sb("tri", [P, P], BF16)
        ones_bf = sb("ones_bf", [P, P], BF16)
        gate_raw = sb("gate_raw", [P, 2])
        gate = sb("gate", [P, 2])
        bv_sb = sb("bv_sb", [P, KT])
        bo_sb = sb("bo_sb", [1, D])
        ones_f = sb("ones_f", [P, P])
        bias_rows = sb("bias_rows", [P, D], F32R)
        row_pick = sb("row_pick", [P, P], F32R)

        qst = sb("qst", [P, H, S], F32R)
        kst = sb("kst", [P, H, S], F32R)
        v_in = sb("v_in", [P, KB, HALF * HD])
        v_sb = [sb(f"v_{i}", [P, KB, HALF * VW + P - VW], F32R) for i in range(2)]
        m_cols = sb("m_cols", [P, 2, KB])
        p_full = sb("p_full", [P, KB, S])
        p_hi = sb("p_hi", [P, KB, S], F32R)
        p_lo = sb("p_lo", [P, KB, S], F32R)
        staged = sb("staged", [VW, 2, S])
        o_by_hi = sb("o_by_hi", [P, S])
        o_by_lo = sb("o_by_lo", [P, S])
        sums = sb("sums", [P, 2, S])
        recip = sb("recip", [P, S])
        o_t = sb("o_t", [P, S])
        ot_hi = sb("ot_hi", [P, NG, S], F32R)
        ot_lo = sb("ot_lo", [P, NG, S], F32R)
        x_res = sb("x_res", [P, TT, D])
        x1 = x_res
        zero_rows = x_res[:, 0:2, :]
        bv_wide = x_res[:, 2, :].rearrange("p (k c) -> p k c", c=P)
        stats = sb("stats2", [P, TT, 6])
        small = sb("small", [P, 8, TT])
        neg_half = sb("neg_half2", [P, TT])
        xr = sb("xr", [P, TT, RW])
        x2t = wo_raw
        logits_t = sb("logits_t", [E, S])
        rt = sb("rt", [P, 12, TT, E])
        r4 = sb("r4", [P, 10, TT])
        mask = sb("mask", [P, TT, E], BF16)
        tok_id = sb("tok_id", [P, TT])
        carry = sb("carry", [P, E])
        slot_u = sb("slot_u", [P, 2, TT], U32)

        def ps(name, shape):
            return ctx.enter_context(nc.psum_tensor(name, shape, F32))

        smax_ps = ps("smax_ps", [P, 2, S])
        st_ps = ps("st_ps", [P, 2, S])
        pv_ps = ps("pv_ps", [P, 2, S])
        work_ps = ps("work_ps", [P, S])
        turn_ps = ps("turn_ps", [P, S])

        const_loaded = sem("const_loaded")
        const_ready = sem("const_ready")
        bias_ps_ready = sem("bias_ps_ready")
        smax_done = sem("smax_done")
        max_done = sem("max_done")
        m_turned = sem("m_turned")
        m_row_ready = sem("m_row_ready")
        st_done = sem("st_done")
        exp_done = sem("exp_done")
        p_lo_dve = sem("p_lo_dve")
        p_lo_pool = sem("p_lo_pool")
        p_used = sem("p_used")
        group_begun = sem("group_begun")
        o_staged = sem("o_staged")
        o_summed = sem("o_summed")
        recip_done = sem("recip_done")
        o_norm_ready = sem("o_norm_ready")
        ot_hi_ready = sem("ot_hi_ready")
        ot_lo_ready = sem("ot_lo_ready")
        x_res_loaded = sem("x_res_loaded")
        o_projected = sem("o_projected")
        x1_ready = sem("x1_ready")
        x1_stored = sem("x1_stored")
        stats2_ready = sem("stats2_ready")
        ln_step = sem("ln_step")
        var_eps2_ready = sem("var_eps2_ready")
        rstd2_ready = sem("rstd2_ready")
        xn2_ready = sem("xn2_ready")
        xn2_turned = sem("xn2_turned")
        x2t_ready = sem("x2t_ready")
        gated = sem("gated")
        logits_t_ready = sem("logits_t_ready")
        logits_turned = sem("logits_turned")
        route_step = sem("route_step")
        shifted_ready = sem("shifted_ready")
        exp_gate_ready = sem("exp_gate_ready")
        mask_ready = sem("mask_ready")
        ranked = sem("ranked")
        slots_ready = sem("slots_ready")
        rows_sent = sem("rows_sent")
        rows_stored = sem("rows_stored")
        pads_stored = sem("pads_stored")
        counts_stored = sem("counts_stored")
        const_set = sem("const_set")
        gate_ready = sem("gate_ready")
        bias_ready = sem("bias_ready")
        stack_loaded = [sem(f"stack_loaded_{g}") for g in range(NG)]
        v_loaded = sem("v_loaded")
        v_hi_ready = sem("v_hi_ready")
        v_lo_ready = sem("v_lo_ready")
        stacked = [sem(f"stacked_{i}") for i in range(2)]

        def at_least(eng, semaphore, value):
            if not (isinstance(value, int) and value <= 0):
                eng.wait_ge(semaphore, value)

        def f32(ap):
            return ap.bitcast(F32)

        def head_exists(b, h):
            if isinstance(b, int):
                return 0 <= H * b + h < H * B
            return True

        def past_first(b):
            return not isinstance(b, int) or b >= 2

        def wait_lo(eng, w, kb):
            if kb in DVE_LO:
                eng.wait_ge(p_lo_dve, len(DVE_LO) * w + DVE_LO.index(kb) + 1)
            else:
                others = [k for k in range(KB) if k not in DVE_LO]
                eng.wait_ge(p_lo_pool, len(others) * w + others.index(kb) + 1)

        def make_lo(eng, w, kb):
            eng.wait_ge(exp_done, KB * w + kb + 1)
            eng.tensor_tensor(p_lo[:, kb, :], p_full[:, kb, :], f32(p_hi[:, kb, :]), ALU.subtract).then_inc(
                p_lo_dve if kb in DVE_LO else p_lo_pool, 1)

        def v_part(i, part):
            return v_sb[i][:, :, 0:HALF * VW].rearrange("p k (h c) -> p k h c", c=VW)[:, :, :, part * HD:part * HD + HD]

        def group_exists(b, n):
            return not isinstance(b, int) or 0 <= NG * b + n < NG * B

        PROJECT_AT = [divmod(27 + 4 * t + g, KB) for t in range(TT) for g in range(NG)]
        RESIDUAL_AT = [divmod(31 + 4 * t, KB) for t in range(TT)]
        MOMENTS_AT, *NORM_AT = [divmod(44 + n, KB) for n in range(3)]
        TURN_AT = [divmod(48 + k, KB) for k in range(KT)]
        X2T_AT = [divmod(48 + k, KB) for k in range(KT)]
        LOGITS_AT = [divmod(52 + 2 * k, KB) for k in range(KT)]
        TAKE_LOGITS_AT, TURN_LOGITS_AT, SCORES_AT, EXP_AT, MASK_AT = [divmod(59 + n, KB) for n in range(5)]
        RANK_AT, SLOTS_AT = (0, 3), (1, 1)

        block = ctx.enter_context(nc.Block())

        def run(eng, slot):
            for b in range(2):
                for h in range(H):
                    slot(b, h)
            with eng.Fori(2, B) as b:
                for h in range(H):
                    slot(b, h)
            for h in range(H):
                slot(B, h)
            for h in range(2):
                slot(B + 1, h)

        @block.sync
        def _(sp):
            for dst, src in ((wo_raw[:], wo_t.rearrange("(k p) n -> p k n", p=P)),
                             (gw[:], gate_w_t.rearrange("(k p) e -> p k e", p=P)),
                             (cst[:], consts), (gate_raw[:], gates), (bv_sb[:], bv), (bo_sb[:], bo)):
                sp.dma_start(dst, src).then_inc(const_loaded, 16)

            def load_stacks(b, h):
                q_h, k_h = [parts[b, h:h + 2].rearrange("h c r s -> (c r) h s") for parts in (q_parts, k_parts)]
                hs = slice(h, h + 2)
                for dst, src in ((qst[0:2 * HD, hs, :], q_h), (qst[2 * HD:SK, hs, :], q_h[0:HD]),
                                 (kst[0:HD, hs, :], k_h[0:HD]), (kst[HD:SK, hs, :], k_h)):
                    sp.dma_start(f32(dst), src).then_inc(stack_loaded[h // GH], 16)

            def load_v(b, i):
                src = v_raw[b].rearrange("(k p) d -> p k d", p=P)[:, :, i * HALF * HD:(i + 1) * HALF * HD]
                sp.dma_start(v_in[:], src).then_inc(v_loaded, 16)

            for h in range(0, H, 2):
                load_stacks(0, h)
            load_v(0, 0)
            sp.wait_ge(const_set, 1)
            sp.dma_start(x1_rows[B * S:B * S + 2 * P, :].rearrange("(p j) d -> p (j d)", j=2), zero_rows.rearrange("p j d -> p (j d)")).then_inc(pads_stored, 16)

            def slot(b, h, prefetch=True):
                first, tail = isinstance(b, int) and b == 0, isinstance(b, int) and b >= B
                u, c = H * b + h, b - 1
                if h == 0 and not first:
                    if isinstance(b, int) and b == 1:
                        sp.wait_ge(pads_stored, 16)
                        sp.wait_ge(gated, 1)
                    else:
                        sp.wait_ge(x1_stored, 16 * (b - 1))
                    sp.dma_start(x_res[:], x[c].rearrange("(t p) d -> p t d", p=P)).then_inc(x_res_loaded, 16)
                def stack_head():
                    z, j = u - 4, (h - 4) % GH
                    if j == 0:
                        at_least(sp, o_summed, NG * b + h // GH - 1)
                        sp.sem_inc(group_begun, 1)
                    sp.wait_ge(o_staged, z + 1)
                    for part, dst in enumerate((o_by_hi[:], o_by_lo[:], sums[:, (h // GH + 1) % 2, :])):
                        sp.dma_start(dst[HD * j:HD * j + HD, :], staged[HD * part:HD * part + HD, h % 2, :]).then_inc(stacked[h % 2], 16)

                if head_exists(b, h - 4) and h % GH != 0:
                    stack_head()
                if head_exists(b, h - 4) and h % GH == 0:
                    stack_head()
                if not first and not tail and h in (0, 2):
                    sp.wait_ge(st_done, KB * (u - 2))
                    load_stacks(b, H + h - 4)
                if h >= 4 and h % 2 == 0 and not tail and prefetch:
                    sp.wait_ge(st_done, KB * (u - 2))
                    load_stacks(b + 1, h - 4)
                if not tail and h == 3:
                    sp.wait_ge(v_lo_ready, 2 * b + 1)
                    load_v(b, 1)
                if h == 12 and not first:
                    sp.wait_ge(xn2_ready, TT * b)
                    sp.dma_start(x1_rows[bass.ds(c * S, S), :].rearrange("(t p) d -> p t d", p=P), x1[:]).then_inc(x1_stored, 16)
                if h == 11 and not tail and prefetch:
                    sp.wait_ge(v_lo_ready, 2 * b + 2)
                    load_v(b + 1, 0)

            for b in range(2):
                for h in range(H):
                    slot(b, h)
            with sp.Fori(2, B - 1) as b:
                for h in range(H):
                    slot(b, h)
            for h in range(H):
                slot(B - 1, h, prefetch=False)
            for h in range(H):
                slot(B, h)
            sp.wait_ge(slots_ready, B)
            sp.dma_start(counts, carry[0:1, :]).then_inc(counts_stored, 16)
            sp.wait_ge(counts_stored, 16)
            sp.wait_ge(pads_stored, 16)
            sp.wait_ge(x1_stored, 16 * B)
            sp.wait_ge(rows_stored, 2 * TT * 16 * B)

        @block.gpsimd
        def _(pool):
            pool.memset(neg_half[:], -0.5).then_inc(const_ready, 1)
            pool.memset(zero_rows, 0.0).then_inc(const_set, 1)
            pool.wait_ge(const_ready, 1)
            pool.wait_ge(const_set, 1)
            pool.memset(f32(kst[SK:SK + KB, :, :]), 1.0).then_inc(const_ready, 1)
            pool.wait_ge(const_ready, 2)
            for i in range(2):
                pool.memset(f32(v_sb[i][:]), 1.0).then_inc(const_ready, 1)
            pool.wait_ge(const_ready, 4)

            def slot(b, h):
                first, tail = isinstance(b, int) and b == 0, isinstance(b, int) and b >= B
                c = b - 1
                G = NG * b + h // GH - 2
                for kb in range(KB):
                    if group_exists(b, h // GH - 2):
                        if h % GH == 0 and kb == 0:
                            pool.wait_ge(stacked[0], 96 * (G + 1))
                            pool.wait_ge(stacked[1], 96 * (G + 1))
                            at_least(pool, ot_lo_ready, G)
                            pool.tensor_tensor(o_t[:], o_by_hi[:], o_by_lo[:], ALU.add).then_inc(o_summed, 1)
                        if h % GH == 1 and kb == 3:
                            pool.wait_ge(recip_done, KB * (G + 1))
                            pool.wait_ge(o_summed, G + 1)
                            pool.tensor_tensor(o_t[:], o_t[:], recip[:], ALU.mult).then_inc(o_norm_ready, 1)
                        if h % GH == 3 and kb == 0:
                            g = (h // GH - 2) % NG
                            pool.wait_ge(ot_hi_ready, G + 1)
                            pool.tensor_tensor(ot_lo[:, g, :], o_t[:], f32(ot_hi[:, g, :]), ALU.subtract).then_inc(ot_lo_ready, 1)
                    if head_exists(b, h - 2) and kb not in DVE_LO:
                        make_lo(pool, H * b + h - 2, kb)
                    if (h, kb) == MOMENTS_AT and not first:
                        pool.wait_ge(var_eps2_ready, b)
                        pool.tensor_tensor(small[:, 7, :], small[:, 6, :], neg_half[:], ALU.pow).then_inc(rstd2_ready, 1)
                if 2 <= h < 2 + 2 * TT and past_first(b):
                    send_rows(b - 2, h - 2)

            def send_rows(c, n):
                if n == 0:
                    pool.wait_ge(slots_ready, c + 1)
                    pool.sem_inc(rows_sent, 1)
                pool.indirect_dma_start(rows, bass.IndirectOffsetOnAxis(slot_u[:, n // TT, n % TT:n % TT + 1], 0),
                                        xr[:, n % TT, :], None).then_inc(rows_stored, 16)

            run(pool, slot)
            for n in range(2 * TT):
                send_rows(B - 1, n)

        @block.scalar
        def _(act):
            act.wait_ge(const_loaded, 96)
            act.activation(wo_hi[:], wo_raw[:], ACT.Copy).then_inc(gate_ready, 1)
            act.activation(gate[:], gate_raw[:], ACT.Tanh).then_inc(gate_ready, 1)
            act.wait_ge(const_ready, 4)

            def slot(b, h):
                first, tail = isinstance(b, int) and b == 0, isinstance(b, int) and b >= B
                u, c = H * b + h, b - 1
                for kb in range(KB):
                    if head_exists(b, h - 2):
                        w = u - 2
                        act.wait_ge(st_done, KB * w + kb + 1)
                        act.activation(p_full[:, kb, :], st_ps[:, kb % 2, :], ACT.Exp, scale=SCALE)
                        act.activation(p_hi[:, kb, :], st_ps[:, kb % 2, :], ACT.Exp, scale=SCALE).then_inc(exp_done, 1)
                    if kb == 1:
                        if h in (1, 5) and not tail:
                            i = h // 4
                            act.wait_ge(v_loaded, 16 * (2 * b + i + 1))
                            at_least(act, p_used, KB * (H * b - HALF * (1 - i)))
                            act.activation(v_part(i, 0), v_in[:].rearrange("p k (h c) -> p k h c", c=HD), ACT.Copy).then_inc(v_hi_ready, 1)
                    if kb == 3 and h % GH == 2 and group_exists(b, h // GH - 2):
                        g = (h // GH - 2) % NG
                        act.wait_ge(o_norm_ready, NG * b + h // GH - 1)
                        at_least(act, o_projected, TT * (b - 1) if g >= 2 else TT * b)
                        act.activation(ot_hi[:, g, :], o_t[:], ACT.Copy).then_inc(ot_hi_ready, 1)
                    if not first and (h, kb) in X2T_AT:
                        x2t_copy(b, X2T_AT.index((h, kb)))
                    if (h, kb) == EXP_AT and not first:
                        act.wait_ge(shifted_ready, b)
                        act.activation(rt[:, 1], rt[:, 0], ACT.Exp).then_inc(exp_gate_ready, 1)
                if head_exists(b, h - 3):
                    y = u - 3
                    act.wait_ge(p_used, KB * (y + 1))
                    at_least(act, stacked[(h - 3) % 2], 48 * ((H * b + h - 3) // 2) if isinstance(b, int) else b * (48 * H // 2) + 48 * ((h - 3) // 2))
                    act.activation(staged[:, (h - 3) % 2, :], pv_ps[0:VW, (h - 3) % 2, :], ACT.Copy).then_inc(o_staged, 1)

            def x2t_copy(b, k):
                act.wait_ge(xn2_turned, KT * (b - 1) + k + 1)
                act.activation(x2t[:, k, :], work_ps[:], ACT.Copy).then_inc(x2t_ready, 1)

            run(act, slot)

        @block.vector
        def _(dve):
            dve.wait_ge(gate_ready, 2)
            dve.wait_ge(const_loaded, 96)
            dve.tensor_tensor(wo_lo[:], wo_raw[:], f32(wo_hi[:]), ALU.subtract).then_inc(bias_ps_ready, 1)
            dve.tensor_copy(tri[:], tri_f).then_inc(bias_ps_ready, 1)
            dve.memset(ones_bf[:], 1.0).then_inc(bias_ps_ready, 1)
            dve.memset(ones_f[:], 1.0).then_inc(bias_ps_ready, 1)
            dve.tensor_copy(tok_id[:], cst[:, 2 * P + TT * E:2 * P + TT * E + TT]).then_inc(bias_ps_ready, 1)
            dve.tensor_copy(carry[:], cst[:, 2 * P + TT * E + TT:2 * P + TT * E + TT + E]).then_inc(bias_ps_ready, 1)
            dve.memset(f32(bias_rows[:]), 0.0).then_inc(bias_ps_ready, 1)
            dve.memset(f32(row_pick[:]), 0.0).then_inc(bias_ps_ready, 1)
            dve.wait_ge(bias_ps_ready, 8)
            for row in (0, HD):
                dve.memset(f32(row_pick[row:row + 1, :]), 1.0).then_inc(bias_ps_ready, 1)
            for k in range(KT):
                dve.tensor_scalar(bv_wide[:, k, :], ones_f[:], bv_sb[:, k:k + 1], None, ALU.mult).then_inc(bias_ps_ready, 1)
            dve.wait_ge(gated, 1)
            dve.tensor_copy(bias_rows[0:HD, :], work_ps[0:HD, :]).then_inc(bias_ready, 1)
            dve.wait_ge(bias_ready, 1)
            dve.tensor_tensor(bias_rows[HD:2 * HD, :], work_ps[0:HD, :], f32(bias_rows[0:HD, :]), ALU.subtract).then_inc(bias_ready, 1)

            LN_STEPS = 6
            RT_STEPS = 26

            def slot(b, h):
                first, tail = isinstance(b, int) and b == 0, isinstance(b, int) and b >= B
                u, c = H * b + h, b - 1
                for kb in range(KB):
                    if not tail:
                        dve.wait_ge(smax_done, KB * u + kb + 1)
                        if kb == 0:
                            at_least(dve, m_turned, u - 1)
                        dve.tensor_reduce(m_cols[:, h % 2, kb:kb + 1], smax_ps[:, kb % 2, :], AX_X, ALU.max).then_inc(max_done, 1)
                    if kb == 1 and head_exists(b, h - 1):
                        dve.wait_ge(m_turned, u)
                        maxima = turn_ps[0:KB, 0:P].unsqueeze(1).to_broadcast([KB, KB, P])
                        own = cst[0:KB, 0:KB].unsqueeze(2).to_broadcast([KB, KB, P])
                        rows_m = qst[SK:SK + KB, (h - 1) % H, :].rearrange("r (c q) -> r c q", q=P)
                        dve.scalar_tensor_tensor(rows_m, maxima, -1.0, own, ALU.mult, ALU.mult).then_inc(m_row_ready, 1)
                    if not tail and h in (1, 5) and kb == 2:
                        i = h // 4
                        dve.wait_ge(v_hi_ready, 2 * b + i + 1)
                        dve.tensor_tensor(v_part(i, 1), v_in[:].rearrange("p k (h c) -> p k h c", c=HD), f32(v_part(i, 0)), ALU.subtract).then_inc(v_lo_ready, 1)
                    if h % GH in (0, 1) and kb in (0, 1) and group_exists(b, h // GH - 2):
                        G = NG * b + h // GH - 2
                        part = 2 * (h % GH) + kb
                        if part == 0:
                            dve.wait_ge(stacked[0], 96 * (G + 1))
                            dve.wait_ge(stacked[1], 96 * (G + 1))
                            at_least(dve, o_norm_ready, G)
                        blk = slice(part * P, part * P + P)
                        dve.reciprocal(recip[:, blk], sums[:, (h // GH) % 2, blk]).then_inc(recip_done, 1)
                    if (kb - 1) % KB in DVE_LO and head_exists(b, h - 2 - (kb == 0)):
                        make_lo(dve, H * b + h - 2 - (kb == 0), (kb - 1) % KB)
                    if not first:
                        if (h, kb) in RESIDUAL_AT:
                            residual(b, RESIDUAL_AT.index((h, kb)))
                        if (h, kb) == MOMENTS_AT:
                            moments(b)
                        if (h, kb) in NORM_AT:
                            n = 2 * NORM_AT.index((h, kb))
                            norm2(b, range(n, n + 2))
                        if (h, kb) == TAKE_LOGITS_AT:
                            dve.wait_ge(gated, b + 1)
                            at_least(dve, logits_turned, c)
                            dve.tensor_copy(logits_t[:], work_ps[0:E, :]).then_inc(logits_t_ready, 1)
                        if (h, kb) == SCORES_AT:
                            route_scores(b)
                        if (h, kb) == MASK_AT:
                            route_mask(b)
                    if (h, kb) == SLOTS_AT and past_first(b):
                        route_slots(b - 1)
            def residual(b, t):
                n = TT * (b - 1) + t + 1
                dve.wait_ge(o_projected, n)
                if t == 0:
                    dve.wait_ge(x_res_loaded, 16 * b)
                dve.scalar_tensor_tensor(x1[:, t, :], work_ps[:], gate[:, 0:1], x_res[:, t, :], ALU.mult, ALU.add).then_inc(x1_ready, 1)
                dve.wait_ge(x1_ready, n)
                dve.bn_stats(stats[:, t], x1[:, t, :]).then_inc(stats2_ready, 1)

            def moments(b):
                c = b - 1
                dve.wait_ge(stats2_ready, TT * b)
                even, odd = stats[:, :, 0:3], stats[:, :, 3:6]
                dve.tensor_tensor(small[:, 0], even[:, :, 1], odd[:, :, 1], ALU.add).then_inc(ln_step, 1)
                dve.tensor_tensor(small[:, 1], even[:, :, 1], odd[:, :, 1], ALU.subtract).then_inc(ln_step, 1)
                dve.tensor_tensor(small[:, 2], even[:, :, 2], odd[:, :, 2], ALU.add).then_inc(ln_step, 1)
                dve.wait_ge(ln_step, LN_STEPS * c + 3)
                dve.tensor_scalar(small[:, 3], small[:, 0], 0.5, None, ALU.mult).then_inc(ln_step, 1)
                dve.tensor_tensor(small[:, 4], small[:, 1], small[:, 1], ALU.mult).then_inc(ln_step, 1)
                dve.tensor_scalar(small[:, 5], small[:, 2], 1.0 / D, EPS, ALU.mult, ALU.add).then_inc(ln_step, 1)
                dve.wait_ge(ln_step, LN_STEPS * b)
                dve.scalar_tensor_tensor(small[:, 6], small[:, 4], 0.25, small[:, 5], ALU.mult, ALU.add).then_inc(var_eps2_ready, 1)

            def norm2(b, blocks):
                if 0 in blocks:
                    dve.wait_ge(rstd2_ready, b)
                    at_least(dve, rows_stored, 2 * TT * 16 * (b - 1))
                for t in blocks:
                    dve.tensor_scalar(xr[:, t, 0:D], x1[:, t, :], small[:, 3, t:t + 1], small[:, 7, t:t + 1],
                                      ALU.subtract, ALU.mult).then_inc(xn2_ready, 1)

            def wide(ap):
                return ap.unsqueeze(2).to_broadcast([P, TT, E])

            def step_of(b):
                n = [0]

                def step(ins):
                    n[0] += 1
                    ins.then_inc(route_step, 1)

                def done():
                    dve.wait_ge(route_step, RT_STEPS * (b - 1) + n[0])
                return step, done, n

            def route_scores(b):
                step, done, n = step_of(b)
                dve.wait_ge(logits_turned, b)
                logits = work_ps[:, 0:TT * E].rearrange("p (t e) -> p t e", e=E)
                step(dve.tensor_reduce(r4[:, 0], logits, AX_X, ALU.max))
                done()
                dve.tensor_tensor(rt[:, 0], logits, wide(r4[:, 0]), ALU.subtract).then_inc(shifted_ready, 1)
                assert n[0] == 1

            def route_mask(b):
                step, done, n = step_of(b)
                n[0] = 1
                dve.wait_ge(exp_gate_ready, b)
                step(dve.tensor_reduce(r4[:, 1], rt[:, 1], AX_X, ALU.add)); done()
                step(dve.reciprocal(r4[:, 2], r4[:, 1])); done()
                step(dve.tensor_tensor(rt[:, 2], rt[:, 1], wide(r4[:, 2]), ALU.mult)); done()
                prob = rt[:, 2]
                step(dve.tensor_reduce(r4[:, 3], prob, AX_X, ALU.max)); done()
                step(dve.tensor_tensor(rt[:, 3], prob, wide(r4[:, 3]), ALU.is_equal)); done()
                step(dve.tensor_tensor(rt[:, 4], rt[:, 3], rev, ALU.mult)); done()
                step(dve.tensor_reduce(r4[:, 4], rt[:, 4], AX_X, ALU.max)); done()
                step(dve.tensor_tensor(rt[:, 5], rt[:, 4], wide(r4[:, 4]), ALU.is_equal)); done()
                step(dve.scalar_tensor_tensor(rt[:, 6], rt[:, 5], -2.0, prob, ALU.mult, ALU.add)); done()
                step(dve.tensor_reduce(r4[:, 5], rt[:, 6], AX_X, ALU.max)); done()
                step(dve.tensor_tensor(rt[:, 7], rt[:, 6], wide(r4[:, 5]), ALU.is_equal)); done()
                step(dve.tensor_tensor(rt[:, 8], rt[:, 7], rev, ALU.mult)); done()
                step(dve.tensor_reduce(r4[:, 6], rt[:, 8], AX_X, ALU.max)); done()
                step(dve.tensor_tensor(rt[:, 9], rt[:, 8], wide(r4[:, 6]), ALU.is_equal)); done()
                step(dve.tensor_tensor(rt[:, 10], rt[:, 5], rt[:, 9], ALU.add)); done()
                dve.tensor_copy(mask[:], rt[:, 10]).then_inc(mask_ready, 1)
                pairs = xr[:, :, D:D + 2 * E].rearrange("p t (e c) -> p t e c", c=2)
                step(dve.scalar_tensor_tensor(pairs[:, :, :, 1], prob, gate[:, 1:2], rt[:, 10], ALU.mult, ALU.mult))
                step(dve.tensor_copy(pairs[:, :, :, 0], wide(tok_id[:])))
                done()
                step(dve.tensor_scalar(tok_id[:], tok_id[:], float(S), None, ALU.add))
                assert n[0] == 19, n

            def route_slots(b):
                step, done, n = step_of(b)
                n[0] = 19
                dve.wait_ge(ranked, b)
                ranks = work_ps[:, 0:TT * E].rearrange("p (t e) -> p t e", e=E)
                spread = carry[:].unsqueeze(1).to_broadcast([P, TT, E])
                step(dve.tensor_tensor(rt[:, 11], ranks, spread, ALU.add)); done()
                step(dve.tensor_tensor(carry[:], carry[:], work_ps[:, TT * E:TT * E + E], ALU.add))
                step(dve.tensor_tensor(rt[:, 3], rt[:, 11], rt[:, 5], ALU.mult))
                step(dve.tensor_tensor(rt[:, 4], rt[:, 11], rt[:, 9], ALU.mult)); done()
                step(dve.tensor_reduce(r4[:, 7], rt[:, 3], AX_X, ALU.add))
                step(dve.tensor_reduce(r4[:, 8], rt[:, 4], AX_X, ALU.add)); done()
                step(dve.tensor_copy(slot_u[:, 0], r4[:, 7])); done()
                dve.tensor_copy(slot_u[:, 1], r4[:, 8]).then_inc(slots_ready, 1)
                assert n[0] == RT_STEPS, n

            run(dve, slot)

        @block.tensor
        def _(pe):
            pe.wait_ge(const_loaded, 96)
            pe.wait_ge(bias_ps_ready, 10 + KT)
            for k in range(KT):
                pe.matmul(work_ps[:], bv_wide[:, k, :], wo_raw[:, k, :], start=(k == 0), stop=False)
            pe.matmul(work_ps[:], ones_f[0:1, :], bo_sb[:], start=False, stop=True).then_inc(gated, 1)
            pe.wait_ge(const_ready, 4)

            def slot(b, h):
                first, tail = isinstance(b, int) and b == 0, isinstance(b, int) and b >= B
                u, c = H * b + h, b - 1
                for kb in range(KB):
                    blk = slice(kb * P, kb * P + P)
                    if not tail:
                        if kb == 0 and h % GH == 0:
                            pe.wait_ge(stack_loaded[h // GH], 32 * GH * b + 32 * GH)
                        at_least(pe, max_done, KB * u + kb - 1)
                        pe.matmul(smax_ps[:, kb % 2, :], qst[0:SK, h, blk], kst[0:SK, h, :], start=True, stop=True).then_inc(smax_done, 1)
                    if head_exists(b, h - 3):
                        hy, y = (h - 3) % H, u - 3
                        half, hv = hy // HALF, hy % HALF
                        if kb == 0:
                            if hy == 0:
                                pe.wait_ge(v_lo_ready, 2 * b + 1)
                            if hy == HALF:
                                pe.wait_ge(v_lo_ready, 2 * b + 2)
                            at_least(pe, o_staged, y - 1)
                        wait_lo(pe, y, kb)
                        v_head = v_sb[half][:, kb, hv * VW:hv * VW + P]
                        pe.matmul(pv_ps[:, hy % 2, :], v_head, p_hi[:, kb, :], start=(kb == 0), stop=False)
                        last = pe.matmul(pv_ps[:, hy % 2, :], v_head, p_lo[:, kb, :], start=False, stop=(kb == KB - 1))
                        last.then_inc(p_used, 1)
                    if head_exists(b, h - 2):
                        hw, w = (h - 2) % H, u - 2
                        if kb == 0:
                            pe.wait_ge(m_row_ready, w + 1)
                        at_least(pe, exp_done, KB * w + kb - 1)
                        pe.matmul(st_ps[:, kb % 2, :], kst[0:SK + KB, hw, blk], qst[0:SK + KB, hw, :], start=True, stop=True).then_inc(st_done, 1)
                    if kb == 1 and head_exists(b, h - 1):
                        pe.wait_ge(max_done, KB * u)
                        at_least(pe, m_row_ready, u - 1)
                        pe.transpose(turn_ps[0:KB, 0:P], m_cols[:, (h - 1) % 2, :], ident).then_inc(m_turned, 1)
                    if not first:
                        if (h, kb) in PROJECT_AT:
                            n = PROJECT_AT.index((h, kb))
                            out_projection(b, n // NG, n % NG)
                        if (h, kb) in TURN_AT:
                            turn_x2(b, TURN_AT.index((h, kb)))
                        if (h, kb) in LOGITS_AT:
                            gate_logits(b, LOGITS_AT.index((h, kb)))
                        if (h, kb) == TURN_LOGITS_AT:
                            turn_logits(b)
                    if (h, kb) == RANK_AT and past_first(b):
                        rank(b - 1)

            def out_projection(b, t, g):
                if g == 0 and t == 0:
                    if isinstance(b, int) and b == 1:
                        pe.wait_ge(bias_ready, 2)
                    at_least(pe, slots_ready, b - 1)
                elif g == 0:
                    pe.wait_ge(x1_ready, TT * (b - 1) + t)
                if t == 0:
                    pe.wait_ge(ot_lo_ready, NG * (b - 1) + g + 1)
                tok = slice(t * P, t * P + P)
                if g == 0:
                    pe.matmul(work_ps[:], row_pick[:], bias_rows[:], start=True, stop=False)
                pe.matmul(work_ps[:], ot_hi[:, g, tok], wo_hi[:, g, :], start=False, stop=False)
                pe.matmul(work_ps[:], ot_lo[:, g, tok], wo_hi[:, g, :], start=False, stop=False)
                last = pe.matmul(work_ps[:], ot_hi[:, g, tok], wo_lo[:, g, :], start=False, stop=(g == NG - 1))
                if g == NG - 1:
                    last.then_inc(o_projected, 1)

            def turn_x2(b, k):
                if k == 0:
                    pe.wait_ge(xn2_ready, TT * b)
                else:
                    pe.wait_ge(x2t_ready, KT * (b - 1) + k)
                for t in range(TT):
                    last = pe.transpose(work_ps[:, t * P:t * P + P], xr[:, t, k * P:k * P + P], ident)
                last.then_inc(xn2_turned, 1)

            def gate_logits(b, k):
                if k == 0:
                    pe.wait_ge(x2t_ready, KT * b)
                last = pe.matmul(work_ps[0:E, :], gw[:, k, :], x2t[:, k, :], start=(k == 0), stop=(k == KT - 1))
                if k == KT - 1:
                    last.then_inc(gated, 1)

            def turn_logits(b):
                pe.wait_ge(logits_t_ready, b)
                for t in range(TT):
                    last = pe.matmul(work_ps[:, t * E:t * E + E], logits_t[:, t * P:t * P + P], cst[0:E, 0:E], start=True, stop=True)
                last.then_inc(logits_turned, 1)

            def rank(b):
                pe.wait_ge(mask_ready, b)
                for t in range(TT):
                    out = work_ps[:, t * E:t * E + E]
                    for before in range(t):
                        pe.matmul(out, ones_bf[:], mask[:, before, :], start=(before == 0), stop=False)
                    pe.matmul(out, tri[:], mask[:, t, :], start=(t == 0), stop=True)
                out = work_ps[:, TT * E:TT * E + E]
                for t in range(TT):
                    last = pe.matmul(out, ones_bf[:], mask[:, t, :], start=(t == 0), stop=(t == TT - 1))
                last.then_inc(ranked, 1)

            run(pe, slot)


def run_experts(nc, rows, counts, w1, w3, w2, ident_dram, first_row, pad_ids, out_rows):
    E, D, HID = w1.shape
    CAP = rows.shape[0] // E
    TB = TILE // P
    KT = D // P
    MB = HID // P
    RING = 4
    CH = 4
    MAX_TILES = (CAP - TILE) // TILE
    ALL_TILES = E * MAX_TILES

    with ExitStack() as ctx:
        def sb(name, shape, dt=F32):
            return ctx.enter_context(nc.sbuf_tensor(name, shape, dt))

        def sem(name):
            return ctx.enter_context(nc.semaphore(name))

        def f32(ap):
            return ap.bitcast(F32)

        up_raw = sb("up_raw", [P, 2, KT, HID])
        up_hi = sb("up_hi", [P, 2, KT, HID], F32R)
        up_lo = sb("up_lo", [P, 2, KT, HID], F32R)
        down_raw = sb("down_raw", [P, MB, D])
        down_hi = sb("down_hi", [P, MB, D], F32R)
        down_lo = sb("down_lo", [P, MB, D], F32R)
        ident = sb("ident_m", [P, P])
        xg = sb("xg", [P, TB, D])
        id_weight = sb("id_weight", [P, TB, 2])
        id_u = sb("id_u", [P, TB], U32)
        xt_hi = sb("xt_hi", [P, KT, TILE], F32R)
        xt_lo = sb("xt_lo", [P, KT, TILE], F32R)
        gated_half = sb("gated_half", [P, 2, TILE])
        h_raw = sb("h_raw", [P, MB, TILE])
        h_hi = sb("h_hi", [P, MB, TILE], F32R)
        h_lo = sb("h_lo", [P, MB, TILE], F32R)
        y = sb("y", [P, TB, D])
        counts_f = sb("counts_f", [1, E])
        first_row_sb = sb("first_row_sb", [1, E])
        pad_ids_sb = sb("pad_ids_sb", [P, TB, 2])
        count_step = sb("count_step", [1, 2, E])
        row_end = sb("row_end", [1, E], I32)
        tiles_i = sb("tiles_i", [1, 2, E], I32)
        tiles = sb("tiles", [1, E], I32)
        pad = sb("pad", [P, TB, RW])
        up_ps = ctx.enter_context(nc.psum_tensor("up_ps", [P, RING, 2, TILE], F32))
        turn_ps = ctx.enter_context(nc.psum_tensor("turn_m_ps", [P, KT, TILE], F32))
        down_ps = ctx.enter_context(nc.psum_tensor("down_ps", [P, TB, D], F32))

        setup_loaded = sem("setup_loaded")
        count_steps = sem("count_steps")
        pad_zeroed = sem("pad_zeroed")
        pads_written = sem("pads_written")
        pads_seen = sem("pads_seen")
        up_loaded = [sem(f"up_loaded_{n}") for n in range(2)]
        down_loaded = sem("down_loaded")
        up_hi_ready = sem("up_hi_ready")
        up_lo_ready = sem("up_lo_ready")
        down_hi_ready = sem("down_hi_ready")
        down_lo_ready = sem("down_lo_ready")
        xg_loaded = sem("xg_loaded")
        id_loaded = sem("id_loaded")
        turned = sem("turned_m")
        xt_hi_ready = sem("xt_hi_ready")
        xt_lo_ready = sem("xt_lo_ready")
        up_done = sem("up_done")
        raw_free = sem("raw_free")
        silu_ready = sem("silu_ready")
        h_made = sem("h_made")
        h_hi_ready = sem("h_hi_ready")
        h_lo_ready = sem("h_lo_ready")
        down_done = sem("down_done")
        y_made = sem("y_made")
        y_seen = sem("y_seen")
        scattered = sem("scattered")
        y_sent = sem("y_sent")
        UP_PARTS = 2 * CH

        block = ctx.enter_context(nc.Block())

        def tile_loops(eng, body, expert=None, peel_last=False):
            r = eng.alloc_register("tiles_before")
            eng.reg_mov(r, 0)

            def one(e):
                if expert:
                    expert(e, eng.snap(r, min_val=0, max_val=ALL_TILES))
                before = eng.snap(r, min_val=0, max_val=ALL_TILES)
                n = eng.value_load(tiles[0:1, bass.ds(e, 1)], min_val=1, max_val=MAX_TILES)
                with eng.Fori(0, n) as i:
                    body(e, i, before + i)
                eng.reg_add(r, r, n)

            with eng.Fori(0, E - 1 if peel_last else E) as e:
                one(e)
            if peel_last:
                one(E - 1)
            return eng.snap(r, min_val=1, max_val=ALL_TILES)

        def load_weights(eng, e):
            for n in range(2):
                cols = slice(n * HID // 2, (n + 1) * HID // 2)
                for i, w in enumerate((w1, w3)):
                    eng.dma_start(up_raw[:, i, :, cols], w[e].rearrange("(k p) n -> p k n", p=P)[:, :, cols]).then_inc(up_loaded[n], 16)
            eng.dma_start(down_raw[:], w2[e].rearrange("(m p) n -> p m n", p=P)).then_inc(down_loaded, 16)

        @block.sync
        def _(sp):
            for dst, src in ((counts_f, counts), (first_row_sb, first_row), (pad_ids_sb, pad_ids), (ident, ident_dram)):
                sp.dma_start(dst[:], src).then_inc(setup_loaded, 16)
            sp.dma_start(id_weight[:], pad_ids).then_inc(id_loaded, 16)
            sp.wait_ge(count_steps, 7)

            def expert(e, f):
                end = sp.value_load(row_end[0:1, bass.ds(e, 1)], min_val=0, max_val=E * CAP - TILE)
                sp.dma_start(rows[bass.ds(end, TILE), :].rearrange("(t p) d -> p t d", p=P), pad[:]).then_inc(pads_written, 16)
                sp.wait_ge(pads_written, e * 16 + 16)
                sp.sem_inc(pads_seen, 1)

            def tile(e, i, f):
                start = e * CAP + i * TILE
                sp.wait_ge(turned, f * 2 + 2)
                sp.dma_start(xg[:], rows[bass.ds(start, TILE), 0:D].rearrange("(t p) d -> p t d", p=P)).then_inc(xg_loaded, 16)
                sp.wait_ge(y_made, f * TB + TB)
                sp.dma_start(id_weight[:], rows[bass.ds(start, TILE), bass.ds(e * 2 + D, 2)].rearrange("(t p) c -> p t c", p=P)).then_inc(id_loaded, 16)

            total = tile_loops(sp, tile, expert)
            sp.wait_ge(turned, total * 2 + 2)
            sp.dma_start(xg[:], rows[0:TILE, 0:D].rearrange("(t p) d -> p t d", p=P)).then_inc(xg_loaded, 16)

        @block.gpsimd
        def _(pool):
            pool.memset(pad[:], 0.0).then_inc(pad_zeroed, 1)
            load_weights(pool, 0)
            pool.sem_inc(y_sent, 2)
            pool.wait_ge(count_steps, 7)

            def tile(e, i, f):
                for t in range(TB):
                    pool.wait_ge(y_made, f * TB + (TB + t + 1))
                    pool.sem_inc(y_seen, 1)
                    pool.indirect_dma_start(out_rows, bass.IndirectOffsetOnAxis(id_u[:, t:t + 1], 0), y[:, t, :], None,
                                            compute_op=ALU.add).then_inc(scattered, 16)
                pool.wait_ge(scattered, f * 32 + 32)
                pool.sem_inc(y_sent, 1)

            def expert(e, f):
                for c in range(CH):
                    ms = slice(c * MB // CH, (c + 1) * MB // CH)
                    pool.wait_ge(down_hi_ready, e * CH + (c + 1))
                    pool.tensor_tensor(down_lo[:, ms, :], down_raw[:, ms, :], f32(down_hi[:, ms, :]), ALU.subtract).then_inc(down_lo_ready, 1)

                if not isinstance(e, int):
                    pool.wait_ge(up_lo_ready, e * UP_PARTS + UP_PARTS)
                    pool.sem_inc(raw_free, 1)
                    pool.wait_ge(down_lo_ready, e * CH + CH)
                    pool.sem_inc(raw_free, 1)
                    load_weights(pool, e + 1)

            tile_loops(pool, tile, expert, peel_last=True)

        @block.scalar
        def _(act):
            act.wait_ge(count_steps, 7)

            def turn_hi(f):
                for j in range(2):
                    act.wait_ge(turned, f * 2 + (2 + j + 1))
                    act.activation(xt_hi[:, 2 * j:2 * j + 2, :], turn_ps[:, 2 * j:2 * j + 2, :], ACT.Copy).then_inc(xt_hi_ready, 1)

            def expert(e, f):
                act.wait_ge(turned, f * 2 + 4)
                W = HID // CH
                for c in range(CH):
                    if c % (CH // 2) == 0:
                        act.wait_ge(up_loaded[c // (CH // 2)], e * 32 + 32)
                    for i in range(2):
                        cols = slice(c * W, c * W + W)
                        act.activation(up_hi[:, i, :, cols], up_raw[:, i, :, cols], ACT.Copy).then_inc(up_hi_ready, 1)
                act.wait_ge(down_done, f * TB + TB)
                act.wait_ge(down_loaded, e * 16 + 16)
                for c in range(CH):
                    ms = slice(c * MB // CH, (c + 1) * MB // CH)
                    act.activation(down_hi[:, ms, :], down_raw[:, ms, :], ACT.Copy).then_inc(down_hi_ready, 1)

            def tile(e, i, f):
                def hi(m):
                    act.wait_ge(h_made, f * MB + (RING + m + 1))
                    if m == 0:
                        act.wait_ge(down_done, f * TB + TB)
                    act.activation(h_hi[:, m, :], h_raw[:, m, :], ACT.Copy).then_inc(h_hi_ready, 1)

                for m in range(MB):
                    act.wait_ge(up_done, f * MB + (m + 1))
                    act.wait_ge(h_made, f * MB + (RING + m - 1))
                    act.activation(gated_half[:, m % 2, :], up_ps[:, m % RING, 0, :], ACT.Silu).then_inc(silu_ready, 1)
                    if m:
                        hi(m - 1)
                hi(MB - 1)
                turn_hi(f + 1)

            turn_hi(0)
            tile_loops(act, tile, expert)

        @block.vector
        def _(dve):
            dve.sem_inc(h_made, RING)
            dve.wait_ge(setup_loaded, 64)
            dve.tensor_tensor(count_step[:, 0], counts_f[:], first_row_sb[:], ALU.subtract).then_inc(count_steps, 1)
            dve.tensor_copy(row_end[:], counts_f[:]).then_inc(count_steps, 1)
            dve.wait_ge(pad_zeroed, 1)
            pairs = pad[:, :, D:D + 2 * E].rearrange("p t (e c) -> p t e c", c=2)
            dve.tensor_copy(pairs[:, :, :, 0], pad_ids_sb[:, :, 0].unsqueeze(2).to_broadcast([P, TB, E])).then_inc(count_steps, 1)
            dve.wait_ge(count_steps, 3)
            dve.tensor_scalar(count_step[:, 1], count_step[:, 0], float(TILE - 1), None, ALU.add).then_inc(count_steps, 1)
            dve.wait_ge(count_steps, 4)
            dve.tensor_copy(tiles_i[:, 0], count_step[:, 1]).then_inc(count_steps, 1)
            dve.wait_ge(count_steps, 5)
            dve.tensor_scalar(tiles_i[:, 1], tiles_i[:, 0], TILE.bit_length() - 1, None, ALU.arith_shift_right).then_inc(count_steps, 1)
            dve.wait_ge(count_steps, 6)
            dve.tensor_scalar(tiles[:], tiles_i[:, 1], 1, None, ALU.max).then_inc(count_steps, 1)
            dve.wait_ge(count_steps, 7)

            def turn_lo(f):
                for j in range(2):
                    dve.wait_ge(xt_hi_ready, f * 2 + (j + 1))
                    dve.tensor_tensor(xt_lo[:, 2 * j:2 * j + 2, :], turn_ps[:, 2 * j:2 * j + 2, :],
                                      f32(xt_hi[:, 2 * j:2 * j + 2, :]), ALU.subtract).then_inc(xt_lo_ready, 1)

            def expert(e, f):
                W = HID // CH
                for c in range(CH):
                    for i in range(2):
                        cols = slice(c * W, c * W + W)
                        dve.wait_ge(up_hi_ready, e * UP_PARTS + (2 * c + i + 1))
                        dve.tensor_tensor(up_lo[:, i, :, cols], up_raw[:, i, :, cols], f32(up_hi[:, i, :, cols]), ALU.subtract).then_inc(up_lo_ready, 1)

            def weigh_before(f):
                dve.wait_ge(id_loaded, f * 16 + 16)
                dve.wait_ge(y_sent, f + 1)
                dve.tensor_copy(id_u[:], id_weight[:, :, 0])
                for t in range(TB):
                    dve.wait_ge(down_done, f * TB + (t + 1))
                    dve.tensor_scalar(y[:, t, :], down_ps[:, t, :], id_weight[:, t, 1:2], None, ALU.mult).then_inc(y_made, 1)

            def tile(e, i, f):
                def lo(m):
                    dve.wait_ge(h_hi_ready, f * MB + (m + 1))
                    dve.tensor_tensor(h_lo[:, m, :], h_raw[:, m, :], f32(h_hi[:, m, :]), ALU.subtract).then_inc(h_lo_ready, 1)

                weigh_before(f)
                for m in range(MB):
                    dve.wait_ge(silu_ready, f * MB + (m + 1))
                    dve.tensor_tensor(h_raw[:, m, :], gated_half[:, m % 2, :], up_ps[:, m % RING, 1, :], ALU.mult).then_inc(h_made, 1)
                    if m:
                        lo(m - 1)
                lo(MB - 1)
                turn_lo(f + 1)

            dve.memset(down_ps[:], 0.0).then_inc(count_steps, 1)
            dve.wait_ge(count_steps, 8)
            turn_lo(0)
            weigh_before(tile_loops(dve, tile, expert))

        @block.tensor
        def _(pe):
            pe.sem_inc(turned, 2)
            pe.sem_inc(down_done, TB)
            pe.wait_ge(count_steps, 7)
            pe.wait_ge(setup_loaded, 64)

            def turn(f):
                pe.wait_ge(xg_loaded, f * 16 + 16)
                for k in range(KT):
                    for t in range(TB):
                        last = pe.transpose(turn_ps[:, k, t * P:t * P + P], xg[:, t, k * P:k * P + P], ident[:])
                    if k % 2:
                        last.then_inc(turned, 1)

            def tile(e, i, f):
                pe.wait_ge(xt_lo_ready, f * 2 + 2)
                for m in range(MB):
                    if m % (MB // CH) == 0:
                        pe.wait_ge(up_lo_ready, e * UP_PARTS + (2 * (m * CH // MB) + 2))
                    pe.wait_ge(h_made, f * MB + (m + 1))
                    cols = slice(m * P, m * P + P)
                    for w in range(2):
                        out = up_ps[:, m % RING, w, :]
                        for k in range(KT):
                            pe.matmul(out, up_hi[:, w, k, cols], xt_hi[:, k, :], start=(k == 0), stop=False)
                            pe.matmul(out, up_lo[:, w, k, cols], xt_hi[:, k, :], start=False, stop=False)
                            last = pe.matmul(out, up_hi[:, w, k, cols], xt_lo[:, k, :], start=False, stop=(k == KT - 1))
                    last.then_inc(up_done, 1)
                turn(f + 1)
                for t in range(TB):
                    pe.wait_ge(y_made, f * TB + (t + 1))
                    tok = slice(t * P, t * P + P)
                    for m in range(MB):
                        if t == 0:
                            if m % (MB // CH) == 0:
                                pe.wait_ge(down_lo_ready, e * CH + (m * CH // MB + 1))
                            pe.wait_ge(h_lo_ready, f * MB + (m + 1))
                        pe.matmul(down_ps[:, t, :], h_hi[:, m, tok], down_hi[:, m, :], start=(m == 0), stop=False)
                        pe.matmul(down_ps[:, t, :], h_lo[:, m, tok], down_hi[:, m, :], start=False, stop=False)
                        last = pe.matmul(down_ps[:, t, :], h_hi[:, m, tok], down_lo[:, m, :], start=False, stop=(m == MB - 1))
                    last.then_inc(down_done, 1)

            turn(0)
            tile_loops(pe, tile)


def build(nc, x, ctx_t, wq_t, wk_t, wv_t, wo_t, bq, bk, bv, bo, gates, gate_w_t, w1, w3, w2, ident, consts, first_row, pad_ids, out_rows):
    B, S, D = x.shape
    E = w1.shape[0]
    capacity = B * S + TILE
    q_parts, k_parts = [nc.dram_tensor(n, [B, HEADS, 2, D // HEADS, S], F32).ap() for n in ("q_parts", "k_parts")]
    v_raw = nc.dram_tensor("v_raw", [B, S, D], F32).ap()
    rows = nc.dram_tensor("rows", [E * capacity, RW], F32).ap()
    counts = nc.dram_tensor("counts", [1, E], F32).ap()
    project_qkv(nc, x, ctx_t, wq_t, wk_t, wv_t, bq, bk, ident, q_parts, k_parts, v_raw)
    attend_and_route(nc, x, q_parts, k_parts, v_raw, wo_t, bv, bo, gates, gate_w_t, consts, out_rows, rows, counts)
    run_experts(nc, rows, counts, w1, w3, w2, ident, first_row, pad_ids, out_rows)


def kernel(x, ctx_1024, g_xattn, g_ffn, L0_xattn_w_q, L0_xattn_b_q, L0_xattn_w_k, L0_xattn_b_k, L0_xattn_w_v,
           L0_xattn_b_v, L0_xattn_w_o, L0_xattn_b_o, L0_ffn_gate_w, L0_ffn_w1, L0_ffn_w2, L0_ffn_w3):
    import numpy as np
    import concourse.bacc as bacc
    from concourse.bass_utils import run_bass_kernel_spmd

    B, S, D = x.shape
    E = L0_ffn_w1.shape[0]
    TT = S // P
    capacity = B * S + TILE

    def columns(b):
        return np.asarray(b).reshape(D // P, P).T

    eye = np.eye(P, dtype=np.float32)
    token = np.arange(P, dtype=np.float32)[:, None] + P * np.arange(TT, dtype=np.float32)
    first_row = capacity * np.arange(E, dtype=np.float32)[None, :]
    consts = np.concatenate([
        eye,
        np.triu(np.ones((P, P), np.float32), 1),
        np.broadcast_to(np.tile(E - np.arange(E, dtype=np.float32), TT), (P, TT * E)),
        token,
        np.broadcast_to(first_row, (P, E)),
    ], axis=1)
    arrays = dict(
        x=x, ctx_t=np.asarray(ctx_1024).transpose(0, 2, 1),
        wq_t=np.asarray(L0_xattn_w_q).T, wk_t=np.asarray(L0_xattn_w_k).T, wv_t=np.asarray(L0_xattn_w_v).T,
        wo_t=np.asarray(L0_xattn_w_o).T,
        bq=columns(L0_xattn_b_q), bk=columns(L0_xattn_b_k), bv=columns(L0_xattn_b_v),
        bo=np.asarray(L0_xattn_b_o)[None, :],
        gates=np.broadcast_to(np.concatenate([np.asarray(g_xattn), np.asarray(g_ffn)])[None, :], (P, 2)),
        gate_w_t=np.asarray(L0_ffn_gate_w).T, w1=L0_ffn_w1, w3=L0_ffn_w3, w2=L0_ffn_w2,
        ident=eye, consts=consts, first_row=first_row,
        pad_ids=np.stack([B * S + token[:, 0:TILE // P], np.zeros((P, TILE // P), np.float32)], axis=2),
    )
    nc = bacc.Bacc("TRN2", target_bir_lowering=False, num_devices=1)
    ins, args = {}, []
    for name, a in arrays.items():
        a = np.ascontiguousarray(a)
        ins[f"in_{name}_dram"] = a
        args.append(nc.dram_tensor(f"in_{name}_dram", a.shape, mybir.dt.from_np(a.dtype), kind="ExternalInput").ap())
    out = nc.dram_tensor("out_0_dram", (B * S + TILE, D), F32, kind="ExternalOutput").ap()
    build(nc, *args, out)
    got = run_bass_kernel_spmd(nc, [ins], core_ids=[0]).results[0]["out_0_dram"]
    return got[:B * S].reshape(B, S, D)
```
